# Optimizing a Trainium2 kernel written in Bass

```python
import numpy as np
import jax
import jax.numpy as jnp

def _softmax(x, axis=-1):
    return jax.nn.softmax(x, axis=axis)

def _gelu(x):
    return jax.nn.gelu(x, approximate=True)

def _silu(x):
    return jax.nn.silu(x)

def _sigmoid(x):
    return jax.nn.sigmoid(x)

def _layernorm(x, axis=-1, eps=1e-05):
    m = jnp.mean(x, axis=axis, keepdims=True)
    v = jnp.var(x, axis=axis, keepdims=True)
    return (x - m) / jnp.sqrt(v + eps)

def _scatter_add(tgt, idx, src, axis=0):
    return tgt.at[idx].add(src)

def _segment_sum(src, seg, n):
    return jax.ops.segment_sum(src, seg, n)
kernel_name = 'mk_seq_preln_d1_jaxref_r8_0f99bd'

def setup_inputs(seed: int=0):
    np.random.seed(seed)
    _w = jnp.asarray

    def _L0_attn_setup():
        import math
        import jax, jax.numpy as jnp
        import numpy as np
        D = 128
        H = 16
        CH = 8
        EPS = 1e-05

        def _layernorm(x, w, b):
            mu = jnp.mean(x, axis=-1, keepdims=True)
            var = jnp.mean((x - mu) ** 2, axis=-1, keepdims=True)
            return (x - mu) * jax.lax.rsqrt(var + EPS) * w + b

        def _token_diffusion(x, Wqk, Wv, Wo, tau):
            b, n, d = x.shape
            dh = d // H
            qk = (x @ Wqk).reshape(b, n, H, dh).transpose(0, 2, 1, 3)
            v = (x @ Wv).reshape(b, n, H, dh).transpose(0, 2, 1, 3)
            dot = jnp.einsum('bhnd,bhmd->bhnm', qk, qk)
            q2 = jnp.sum(qk * qk, axis=-1)
            logits = (2.0 * dot - q2[..., :, None] - q2[..., None, :]) / math.sqrt(dh)
            logits = logits * tau
            attn = jax.nn.softmax(logits, axis=-1)
            out = jnp.einsum('bhnm,bhmd->bhnd', attn, v)
            out = out.transpose(0, 2, 1, 3).reshape(b, n, d)
            return out @ Wo

        def _channel_diffusion(x, Wqk, Wv, Wo, tau):
            b, n, d = x.shape
            dh = d // CH
            qk = (x @ Wqk).transpose(0, 2, 1).reshape(b, CH, dh, n)
            v = (x @ Wv).transpose(0, 2, 1).reshape(b, CH, dh, n)
            dot = jnp.einsum('bhcn,bhdn->bhcd', qk, qk)
            q2 = jnp.sum(qk * qk, axis=-1)
            logits = (2.0 * dot - q2[..., :, None] - q2[..., None, :]) / math.sqrt(n)
            logits = logits * tau
            attn = jax.nn.softmax(logits, axis=-1)
            out = jnp.einsum('bhcd,bhdn->bhcn', attn, v)
            out = out.reshape(b, d, n).transpose(0, 2, 1)
            return out @ Wo
        key = jax.random.key(seed)
        ks = jax.random.split(key, 8)
        s = 1.0 / math.sqrt(D)
        inp = {'x': jax.random.normal(ks[0], (8, 128, D), dtype=jnp.float32), 'Wqk_t': jax.random.normal(ks[1], (D, D), dtype=jnp.float32) * s, 'Wv_t': jax.random.normal(ks[2], (D, D), dtype=jnp.float32) * s, 'Wo_t': jax.random.normal(ks[3], (D, D), dtype=jnp.float32) * s, 'tau_t': jnp.ones((H, 1, 1), dtype=jnp.float32), 'Wqk_c': jax.random.normal(ks[4], (D, D), dtype=jnp.float32) * s, 'Wv_c': jax.random.normal(ks[5], (D, D), dtype=jnp.float32) * s, 'Wo_c': jax.random.normal(ks[6], (D, D), dtype=jnp.float32) * s, 'tau_c': jnp.ones((CH, 1, 1), dtype=jnp.float32), 'ln1_w': jnp.ones((D,), dtype=jnp.float32), 'ln1_b': jnp.zeros((D,), dtype=jnp.float32), 'ln2_w': jnp.ones((D,), dtype=jnp.float32), 'ln2_b': jnp.zeros((D,), dtype=jnp.float32), 'gamma1': 0.0001 * jnp.ones((D,), dtype=jnp.float32), 'gamma2': 0.0001 * jnp.ones((D,), dtype=jnp.float32)}
        return inp
    _L0_attn_in = _L0_attn_setup()

    def _L0_ffn_setup():
        import jax, jax.numpy as jnp
        import numpy as np
        B, S, D = (4, 256, 128)
        E, F = (8, 512)
        key = jax.random.key(seed)
        ks = jax.random.split(key, 5)
        x = jax.random.normal(ks[0], (B, S, D), dtype=jnp.float32)
        switch_w = jax.random.normal(ks[1], (D, E), dtype=jnp.float32) * D ** (-0.5)
        switch_b = jnp.zeros((E,), dtype=jnp.float32)
        w1 = jax.random.normal(ks[2], (E, D, F), dtype=jnp.float32) * D ** (-0.5)
        b1 = jnp.zeros((E, F), dtype=jnp.float32)
        w2 = jax.random.normal(ks[3], (E, F, D), dtype=jnp.float32) * F ** (-0.5)
        b2 = jnp.zeros((E, D), dtype=jnp.float32)
        return {'x': x, 'switch_w': switch_w, 'switch_b': switch_b, 'w1': w1, 'b1': b1, 'w2': w2, 'b2': b2}
    _L0_ffn_in = _L0_ffn_setup()
    _d = {'L0_attn_x': _L0_attn_in['x'], 'L0_attn_Wqk_t': _L0_attn_in['Wqk_t'], 'L0_attn_Wv_t': _L0_attn_in['Wv_t'], 'L0_attn_Wo_t': _L0_attn_in['Wo_t'], 'L0_attn_tau_t': _L0_attn_in['tau_t'], 'L0_attn_Wqk_c': _L0_attn_in['Wqk_c'], 'L0_attn_Wv_c': _L0_attn_in['Wv_c'], 'L0_attn_Wo_c': _L0_attn_in['Wo_c'], 'L0_attn_tau_c': _L0_attn_in['tau_c'], 'L0_attn_ln1_w': _L0_attn_in['ln1_w'], 'L0_attn_ln1_b': _L0_attn_in['ln1_b'], 'L0_attn_ln2_w': _L0_attn_in['ln2_w'], 'L0_attn_ln2_b': _L0_attn_in['ln2_b'], 'L0_attn_gamma1': _L0_attn_in['gamma1'], 'L0_attn_gamma2': _L0_attn_in['gamma2'], 'L0_ffn_switch_w': _L0_ffn_in['switch_w'], 'L0_ffn_switch_b': _L0_ffn_in['switch_b'], 'L0_ffn_w1': _L0_ffn_in['w1'], 'L0_ffn_b1': _L0_ffn_in['b1'], 'L0_ffn_w2': _L0_ffn_in['w2'], 'L0_ffn_b2': _L0_ffn_in['b2']}
    _x0 = _d['L0_attn_x']
    _d['L0_attn_x'] = jax.random.normal(jax.random.fold_in(jax.random.key(seed), 1), (8, 256, 128), dtype=_x0.dtype)
    del _x0
    return _d

def reference(L0_attn_x, L0_attn_Wqk_t, L0_attn_Wv_t, L0_attn_Wo_t, L0_attn_tau_t, L0_attn_Wqk_c, L0_attn_Wv_c, L0_attn_Wo_c, L0_attn_tau_c, L0_attn_ln1_w, L0_attn_ln1_b, L0_attn_ln2_w, L0_attn_ln2_b, L0_attn_gamma1, L0_attn_gamma2, L0_ffn_switch_w, L0_ffn_switch_b, L0_ffn_w1, L0_ffn_b1, L0_ffn_w2, L0_ffn_b2):

    def _L0_attn_ref(x, Wqk_t, Wv_t, Wo_t, tau_t, Wqk_c, Wv_c, Wo_c, tau_c, ln1_w, ln1_b, ln2_w, ln2_b, gamma1, gamma2):
        import math
        import jax, jax.numpy as jnp
        import numpy as np
        D = 128
        H = 16
        CH = 8
        EPS = 1e-05

        def _layernorm(x, w, b):
            mu = jnp.mean(x, axis=-1, keepdims=True)
            var = jnp.mean((x - mu) ** 2, axis=-1, keepdims=True)
            return (x - mu) * jax.lax.rsqrt(var + EPS) * w + b

        def _token_diffusion(x, Wqk, Wv, Wo, tau):
            b, n, d = x.shape
            dh = d // H
            qk = (x @ Wqk).reshape(b, n, H, dh).transpose(0, 2, 1, 3)
            v = (x @ Wv).reshape(b, n, H, dh).transpose(0, 2, 1, 3)
            dot = jnp.einsum('bhnd,bhmd->bhnm', qk, qk)
            q2 = jnp.sum(qk * qk, axis=-1)
            logits = (2.0 * dot - q2[..., :, None] - q2[..., None, :]) / math.sqrt(dh)
            logits = logits * tau
            attn = jax.nn.softmax(logits, axis=-1)
            out = jnp.einsum('bhnm,bhmd->bhnd', attn, v)
            out = out.transpose(0, 2, 1, 3).reshape(b, n, d)
            return out @ Wo

        def _channel_diffusion(x, Wqk, Wv, Wo, tau):
            b, n, d = x.shape
            dh = d // CH
            qk = (x @ Wqk).transpose(0, 2, 1).reshape(b, CH, dh, n)
            v = (x @ Wv).transpose(0, 2, 1).reshape(b, CH, dh, n)
            dot = jnp.einsum('bhcn,bhdn->bhcd', qk, qk)
            q2 = jnp.sum(qk * qk, axis=-1)
            logits = (2.0 * dot - q2[..., :, None] - q2[..., None, :]) / math.sqrt(n)
            logits = logits * tau
            attn = jax.nn.softmax(logits, axis=-1)
            out = jnp.einsum('bhcd,bhdn->bhcn', attn, v)
            out = out.reshape(b, d, n).transpose(0, 2, 1)
            return out @ Wo
        x = x + _token_diffusion(_layernorm(x, ln1_w, ln1_b), Wqk_t, Wv_t, Wo_t, tau_t) * gamma1
        x = x + _channel_diffusion(_layernorm(x, ln2_w, ln2_b), Wqk_c, Wv_c, Wo_c, tau_c) * gamma2
        return x

    def _L0_ffn_ref(x, switch_w, switch_b, w1, b1, w2, b2):
        import jax, jax.numpy as jnp
        import numpy as np
        B, S, D = (4, 256, 128)
        E, F = (8, 512)
        b, s, d = x.shape
        t = x.reshape(-1, d)
        logits = t @ switch_w + switch_b
        route_prob = jax.nn.softmax(logits, axis=-1)
        route_prob_max = jnp.max(route_prob, axis=-1)
        routes = jnp.argmax(route_prob, axis=-1)
        out = jnp.zeros_like(t)
        n_experts = w1.shape[0]
        for e in range(n_experts):
            h = jax.nn.gelu(t @ w1[e] + b1[e])
            y = h @ w2[e] + b2[e]
            mask = (routes == e)[:, None]
            out = jnp.where(mask, y, out)
        out = out * route_prob_max[:, None]
        return out.reshape(b, s, d)
    x = L0_attn_x
    x = x + _L0_attn_ref(_layernorm(x, axis=-1), L0_attn_Wqk_t, L0_attn_Wv_t, L0_attn_Wo_t, L0_attn_tau_t, L0_attn_Wqk_c, L0_attn_Wv_c, L0_attn_Wo_c, L0_attn_tau_c, L0_attn_ln1_w, L0_attn_ln1_b, L0_attn_ln2_w, L0_attn_ln2_b, L0_attn_gamma1, L0_attn_gamma2)
    x = x + _L0_ffn_ref(_layernorm(x, axis=-1), L0_ffn_switch_w, L0_ffn_switch_b, L0_ffn_w1, L0_ffn_b1, L0_ffn_w2, L0_ffn_b2)
    return x

_drawn_inputs = setup_inputs


def setup_inputs(seed=0):
    import zlib

    import numpy as np

    out = dict(_drawn_inputs(seed))
    spreads = {'L0_attn_tau_t': (1.0, 0.6),
     'L0_attn_tau_c': (1.0, 0.2),
     'L0_attn_ln1_w': (1.0, 0.6),
     'L0_attn_ln1_b': (0.0, 2.0),
     'L0_attn_ln2_w': (1.0, 0.6),
     'L0_attn_ln2_b': (0.0, 2.0),
     'L0_attn_gamma1': (9.999999747378752e-05, 0.6),
     'L0_attn_gamma2': (9.999999747378752e-05, 0.6),
     'L0_ffn_switch_b': (0.0, 0.1),
     'L0_ffn_b1': (0.0, 0.604),
     'L0_ffn_b2': (0.0, 0.414)}
    factors = {'L0_attn_Wqk_t': 64.0,
     'L0_attn_Wv_t': 36.079,
     'L0_attn_Wo_t': 41.968,
     'L0_attn_Wv_c': 38.431,
     'L0_attn_Wo_c': 35.697}
    for name, (base, spread) in spreads.items():
        noise = np.random.default_rng([zlib.crc32(name.encode()), seed]).standard_normal(out[name].shape)
        drawn = base * np.exp(spread * noise) if base else spread * noise
        out[name] = jnp.asarray(drawn.astype(out[name].dtype))
    for name, factor in factors.items():
        out[name] = (out[name] * factor).astype(out[name].dtype)
    return out
```

```python
from contextlib import ExitStack

import concourse.bass as bass
from concourse import mybir

P = 128
F32 = mybir.dt.float32
BF16 = mybir.dt.bfloat16
I32 = mybir.dt.int32
ALU = mybir.AluOpType
ACT = mybir.ActivationFunctionType
AX_X = mybir.AxisListType.X

EPS = 1e-5
B, N, D = 8, 256, 128
H, DH = 16, 8
CH, CDH = 8, 16
E, F = 8, 512
T = N // P
TILES = B * T
PAIRS = H // 2
GROUPS = H // 4
SLOT = 64
PIECES = 3
SUMCOL = 6 * DH
NEG = -1.0e30
FT = F // P
MAGIC = float(0x5F3759DF)


class Link:

    def __init__(self, eng, sem):
        self.eng, self.sem, self.n, self.turn, self.per = eng, sem, 0, None, 0

    def loop(self, i, per):
        self.turn, self.per, self.at = i, per, self.n

    def end(self, turns):
        assert self.n - self.at == self.per, self.n - self.at
        self.n, self.turn = self.at + self.per * turns, None

    def value(self):
        return self.n if self.turn is None else self.turn * self.per + self.n

    def mark(self, ins):
        ins.then_inc(self.sem, 1)
        self.n += 1
        return self.value()

    def wait(self, value):
        self.eng.wait_ge(self.sem, value)

    def __call__(self, ins):
        self.wait(self.mark(ins))


def ge(eng, sem, value):
    if not isinstance(value, int) or value > 0:
        eng.wait_ge(sem, value)


def build(nc, x_in, wqk_t, wv_t, wo_t, tau_t, wqk_c, wvT_c, wo_c, tau_c, ln1_w, ln1_b, ln2_w, ln2_b,
          gamma1, gamma2, switch_w, switch_b, w1, b1T, w2, b2, out):
    with ExitStack() as ctx:
        def sb(name, shape, dt=F32):
            return ctx.enter_context(nc.sbuf_tensor(name, shape, dt))

        def sem(name):
            return ctx.enter_context(nc.semaphore(name))

        psum = ctx.enter_context(nc.psum_tensor("psum", [P, 8, 512], F32))
        banks = [psum[:, i, :] for i in range(8)]
        logit_banks = [banks[0:2], banks[2:4]]
        pv_bank = banks[4]
        aux = banks[5:8]
        auxb = [a.bitcast(BF16) for a in aux]

        xin = sb("xin", [P, TILES, D])
        x0 = sb("x0", [P, TILES, D])
        x1 = sb("x1", [P, TILES, D])
        ident = sb("ident", [P, P])
        identb = sb("identb", [P, P], BF16)
        bn6 = sb("bn6", [P, TILES, 6])
        mv = sb("mv", [P, TILES, 2])
        ve = sb("ve", [P, TILES])
        ri = sb("ri", [P, TILES], I32)
        rt = sb("rt", [P, TILES])
        r1 = sb("r1", [P, TILES])
        r2 = sb("r2", [P, TILES])
        wqkv = sb("wqkv", [P, 2 * D])
        wog_t = sb("wog_t", [P, D])
        g1b = sb("g1b", [P, D])
        cols = sb("cols", [P, 8])
        taub = sb("taub", [P, H])
        s2b = sb("s2b", [P, H, DH])
        snegb = sb("snegb", [P, T, H])
        xh = sb("xh", [P, T, D])
        hT = sb("hT", [P, N])
        sq = sb("sq", [P, T, D])
        ra = sb("ra", [P, T * H, DH])
        pf = sb("pf", [P, T * H, DH])
        rb = sb("rb", [P, T * H, DH])
        c0 = sb("c0", [P, T * H])
        cf = sb("cf", [P, T * H])
        rc = sb("rc", [P, T * H])
        ones = sb("ones", [P, T * H])
        stackA = sb("stackA", [P, T * H, SLOT], BF16)
        stackB = sb("stackB", [P, T * H, SLOT], BF16)
        keysT = [sb(f"keysT{p}", [P, PAIRS, N], BF16) for p in range(2)]
        qrysT = [sb(f"qrysT{p}", [P, PAIRS, 2, N], BF16) for p in range(2)]
        vaug = [sb(f"vaug{p}", [P, T, H, 32]) for p in range(2)]
        expo = [sb(f"expo{i}", [P, T, 2, N]) for i in range(4)]
        oT = sb("oT", [P, GROUPS, N])
        rden = sb("rden", [P, T, H])
        on = sb("on", [P, T, H, DH])
        onT = sb("onT", [P, N])
        wqkc = sb("wqkc", [P, D])
        wvTc = sb("wvTc", [P, D])
        wogc = sb("wogc", [P, D])
        g2b = sb("g2b", [P, D])
        mask = sb("mask", [P, D])
        nhalf = sb("nhalf", [P, D])
        GB = 4
        GT = GB * T
        h2T = sb("h2T", [P, GB, N])
        qc = sb("qc", [P, GB, T * D])
        sqc = sb("sqc", [P, GB, T * D])
        lg = sb("lg", [P, GB, D])
        nmx = sb("nmx", [P, GB])
        ssum = sb("ssum", [P, GB])
        rsum = sb("rsum", [P, GB])
        at = sb("at", [P, GB, D])
        atn = sb("atn", [P, GB, D])
        wp = sb("wp", [P, GB, D])
        wpp = sb("wpp", [P, GB, D])
        y = sb("y", [P, TILES, D])
        xx = sb("xx", [P, TILES, D])
        tn = sb("tn", [P, GT, D])
        tT = sb("tT", [P, TILES * P])
        sww = sb("sww", [P, E])
        swb = sb("swb", [P, E])
        rl = sb("rl", [P, TILES, E])
        rmx = sb("rmx", [P, TILES])
        re = sb("re", [P, TILES, E])
        rs = sb("rs", [P, TILES])
        iota8 = sb("iota8", [P, E])
        cand = sb("cand", [P, TILES, E])
        first = sb("first", [P, TILES])
        pw = sb("pw", [P, TILES, E])
        b1s = sb("b1s", [P, E * FT])
        b2b = sb("b2b", [P, E, D])
        w1b = [sb(f"w1b{p}", [P, F]) for p in range(2)]
        w2b = [sb(f"w2b{p}", [P, FT, D]) for p in range(2)]
        hsb = [sb(f"hsb{p}", [P, FT, 512]) for p in range(2)]

        S = {}

        def s(name):
            if name not in S:
                S[name] = sem(name)
            return S[name]

        for name in ("x_first x_rest attn_weights chan_weights moe_weights ident_ready consts_ready pool_link dve_link "
                     "act_link xn_ready xT_ready hT_ready qv_ready v_ready sq_ready q_read sum_ready pieces_ready "
                     "stack_ready stT_ready stT_read logits_ready exp_ready pv_done o_read oT_ready on_ready "
                     "onTp_ready onT_ready proj_ready x1_ready scaled_ready "
                     "xn2_ready x2T_ready h2T_ready qc_ready qc_copied sqc_ready gram_ready lg_ready at_ready atn_ready "
                     "wp_ready wp_copied wpp_ready wpp_copied x2_ready y_ready tn_ready tTp_ready tT_ready rl_ready "
                     "rl_copied rmx_ready re_ready pw_ready ew_loaded0 ew_loaded1 h_ready gelu_ready y2_ready y2_added "
                     "out_written").split():
            s(name)

        block = ctx.enter_context(nc.Block())

        def steps(eng, link, per, step):
            step(0, 0)
            if eng is not None:
                with eng.Fori(0, (B - 2) // 2) as i:
                    if link:
                        link.loop(i, per)
                    step(i * 2 + 1, 1)
                    step(i * 2 + 2, 0)
                if link:
                    link.end((B - 2) // 2)
            step(B - 1, 1)

        has_next = lambda b: not isinstance(b, int) or b + 1 < B
        has_last = lambda b: not isinstance(b, int) or b > 0

        @block.sync
        def _(sp):
            xv = x_in.rearrange("b (t p) d -> p (b t) d", p=P)
            sp.dma_start(xin[:, 0:T, :], xv[:, 0:T, :]).then_inc(s("x_first"), 16)
            sp.dma_start(wqkv[:, 0:D], wqk_t).then_inc(s("attn_weights"), 16)
            sp.dma_start(wqkv[:, D:2 * D], wv_t).then_inc(s("attn_weights"), 16)
            for k, v in enumerate((ln1_w, ln1_b, ln2_w, ln2_b, tau_c)):
                sp.dma_start(cols[:, k:k + 1], v).then_inc(s("attn_weights"), 16)
            sp.dma_start(taub[:, :], tau_t.partition_broadcast(P)).then_inc(s("attn_weights"), 16)
            sp.dma_start(g1b[:, :], gamma1.partition_broadcast(P)).then_inc(s("attn_weights"), 16)
            sp.dma_start(wog_t[:, :], wo_t).then_inc(s("attn_weights"), 16)
            sp.dma_start(xin[:, T:, :], xv[:, T:, :]).then_inc(s("x_rest"), 16)
            sp.dma_start(wqkc[:, :], wqk_c).then_inc(s("chan_weights"), 16)
            sp.dma_start(wvTc[:, :], wvT_c).then_inc(s("chan_weights"), 16)
            sp.dma_start(wogc[:, :], wo_c).then_inc(s("chan_weights"), 16)
            sp.dma_start(g2b[:, :], gamma2.partition_broadcast(P)).then_inc(s("chan_weights"), 16)
            sp.dma_start(sww[:, :], switch_w).then_inc(s("chan_weights"), 16)
            sp.dma_start(swb[:, :], switch_b.partition_broadcast(P)).then_inc(s("chan_weights"), 16)
            sp.dma_start(b1s[:, :], b1T).then_inc(s("moe_weights"), 16)
            sp.dma_start(b2b[:, :, :].rearrange("p e d -> p (e d)"),
                         b2.rearrange("e d -> (e d)").partition_broadcast(P)).then_inc(s("moe_weights"), 16)
            w2v = w2.rearrange("e (t p) d -> e p t d", p=P)
            for e in range(E):
                ge(sp, s("y2_added"), 4 * (e - 1))
                sp.dma_start(w1b[e % 2][:, :], w1[e, :, :]).then_inc(s(f"ew_loaded{e % 2}"), 16)
                sp.dma_start(w2b[e % 2][:, :, :], w2v[e, :, :, :]).then_inc(s(f"ew_loaded{e % 2}"), 16)
            sp.wait_ge(s("y2_added"), E * 4)
            ov = out.rearrange("b (t p) d -> p (b t) d", p=P)
            sp.dma_start(ov, y[:, :, :]).then_inc(s("out_written"), 16)
            sp.wait_ge(s("out_written"), 16)

        @block.gpsimd
        def _(pool):
            link = Link(pool, s("pool_link"))
            pool.memset(ident[:, :], 0.0).then_inc(s("pool_link"), 1)
            pool.memset(identb[:, :], 0.0).then_inc(s("pool_link"), 1)
            link.n = 2
            link.wait(2)
            for m in (ident, identb):
                pool.affine_select(out=m[:, :], in_=m[:, :], compare_op=ALU.not_equal, fill=1.0, base=0,
                                   pattern=[[-1, P]], channel_multiplier=1).then_inc(s("ident_ready"), 1)
            link(pool.memset(ones[:, :], 1.0))
            pool.memset(nhalf[:, :], -0.5).then_inc(s("consts_ready"), 1)
            link(pool.memset(mask[:, :], 0.0))
            mv3 = mask[:, :].rearrange("p (k c) -> p k c", c=CDH)
            link(pool.affine_select(out=mv3, in_=mv3, compare_op=ALU.is_ge, fill=NEG, base=0,
                                    pattern=[[-CDH, CH], [0, CDH]], channel_multiplier=1))
            pool.affine_select(out=mv3, in_=mv3, compare_op=ALU.is_ge, fill=NEG, base=CDH - 1,
                               pattern=[[CDH, CH], [0, CDH]], channel_multiplier=-1).then_inc(s("consts_ready"), 1)
            pool.iota(iota8[:, :], pattern=[[1, E]], base=0, channel_multiplier=0,
                      allow_small_or_imprecise_dtypes=True).then_inc(s("consts_ready"), 1)

            def copy(dst, src):
                return pool.tensor_tensor(dst, src, ones[:, :].unsqueeze(2).broadcast_to([P, T * H, src.shape[2]]), ALU.mult)

            def replicate(n):
                pool.wait_ge(s("sum_ready"), n + 1)
                ge(pool, s("stT_ready"), n * 4)
                link(copy(stackA[:, :, SUMCOL:SUMCOL + 1], cf[:, :].unsqueeze(2)))
                link(pool.tensor_tensor(rc[:, :].unsqueeze(2), cf[:, :].unsqueeze(2),
                                        stackA[:, :, SUMCOL:SUMCOL + 1], ALU.subtract))
                link(copy(stackA[:, :, SUMCOL + 1:SUMCOL + 2], rc[:, :].unsqueeze(2)))
                link(pool.tensor_tensor(stackA[:, :, SUMCOL + 2:SUMCOL + 3], rc[:, :].unsqueeze(2),
                                        stackA[:, :, SUMCOL + 1:SUMCOL + 2], ALU.subtract))
                link(copy(stackB[:, :, SUMCOL + 3:SUMCOL + 6], stackA[:, :, SUMCOL:SUMCOL + 3]))
                pool.wait_ge(s("pieces_ready"), n + 1)
                copy(stackA[:, :, 8:16], stackA[:, :, 0:8])
                pool.tensor_copy(stackA[:, :, 16:24], stackA[:, :, 0:8])
                pool.tensor_copy(stackA[:, :, 32:40], stackA[:, :, 24:32])
                pool.tensor_copy(stackB[:, :, 24:32], stackB[:, :, 0:8])
                pool.tensor_copy(stackB[:, :, 40:48], stackB[:, :, 0:8])
                pool.tensor_copy(stackB[:, :, 32:40], stackB[:, :, 8:16]).then_inc(s("stack_ready"), 1)

            replicate(0)
            steps(pool, link, 10, lambda b, p: replicate(b + 1) if has_next(b) else None)
            for g in range(2):
                pool.wait_ge(s("x1_ready"), B)
                pool.tensor_tensor(xx[:, GT * g:GT * g + GT, :], x1[:, GT * g:GT * g + GT, :],
                                   xin[:, GT * g:GT * g + GT, :], ALU.add).then_inc(s("scaled_ready"), 1)

        @block.scalar
        def _(act):
            def evac_v(n, q):
                act.wait_ge(s("qv_ready"), n + 1)
                ge(act, s("pv_done"), n * 4 - 4)
                act.activation(vaug[q][:, :, :, 0:DH],
                               aux[2][:, :].rearrange("p (t w h d) -> p w t h d", t=T, w=2, d=DH)[:, 1],
                               ACT.Copy).then_inc(s("v_ready"), 1)
                ge(act, s("sum_ready"), n)
                act.activation(sq[:, :, :], aux[2][:, :].rearrange("p (t w) -> p t w", t=T)[:, :, 0:D],
                               ACT.Square).then_inc(s("sq_ready"), 1)

            def exps(b, j):
                act.wait_ge(s("logits_ready"), b * 8 + j + 1)
                ge(act, s("pv_done"), b * 4 + (j - 4) // 2 + 1)
                act.activation(expo[j % 4][:, :, :, :].rearrange("p t e n -> p t (e n)"),
                               lg_view(j % 2), ACT.Exp).then_inc(s("exp_ready"), 1)

            def lg_view(k):
                return psum[:, 2 * k:2 * k + 2, :]

            def evac_onT(m):
                act.wait_ge(s("onTp_ready"), m + 1)
                act.activation(onT[:, :], aux[1][:, 0:N], ACT.Copy).then_inc(s("onT_ready"), 1)

            def step(b, p):
                for j in range(8):
                    exps(b, j)
                    if j == 1 and has_next(b):
                        evac_v(b + 1, 1 - p)
                    if j == 3 and has_last(b):
                        evac_onT(b - 1)

            act.wait_ge(s("consts_ready"), 4)
            evac_v(0, 0)
            steps(act, None, 0, step)
            evac_onT(B - 1)

            for g in range(2):
                for k in range(GB):
                    act.wait_ge(s("qc_ready"), GB * g + k + 1)
                    ge(act, s("gram_ready"), GB * g)
                    act.activation(sqc[:, k, :], banks[2 * k + 1][:, 0:T * D], ACT.Square).then_inc(s("sqc_ready"), 1)
                for k in range(GB):
                    act.wait_ge(s("lg_ready"), GB * g + k + 1)
                    ge(act, s("atn_ready"), GB * g)
                    act.activation(at[:, k, :], lg[:, k, :], ACT.Exp, bias=nmx[:, k:k + 1],
                                   accum_out=ssum[:, k:k + 1]).then_inc(s("at_ready"), 1)
                for k in range(GB):
                    act.wait_ge(s("wp_ready"), GB * g + k + 1)
                    ge(act, s("wpp_ready"), GB * g)
                    act.activation(wp[:, k, :], banks[2 * k + 1][:, 0:D], ACT.Copy).then_inc(s("wp_copied"), 1)
                for k in range(GB):
                    act.wait_ge(s("tTp_ready"), GB * g + k + 1)
                    act.activation(tT[:, (GB * g + k) * N:(GB * g + k + 1) * N], banks[2 * k][:, 0:N],
                                   ACT.Copy).then_inc(s("tT_ready"), 1)
            act.wait_ge(s("rmx_ready"), 1)
            act.activation(re[:, :, :], rl[:, :, :], ACT.Exp).then_inc(s("re_ready"), 1)

            act.wait_ge(s("moe_weights"), 32)
            for e in range(E):
                for c in range(4):
                    q = e * 4 + c
                    ge(act, s("y2_ready"), q - 1)
                    for f in range(FT):
                        act.wait_ge(s("h_ready"), q * FT + f + 1)
                        act.activation(hsb[q % 2][:, f, :], banks[f][:, :], ACT.Gelu_apprx_tanh,
                                       bias=b1s[:, e * FT + f:e * FT + f + 1]).then_inc(s("gelu_ready"), 1)

        @block.vector
        def _(dve):
            link = Link(dve, s("dve_link"))

            def rsqrt(dst, v, a, b_, eps=EPS):
                k = slice(a, b_)
                link(dve.tensor_scalar(ve[:, k], v, eps, None, ALU.add))
                link(dve.tensor_scalar(ri[:, k], ve[:, k].bitcast(I32), 1, None, ALU.arith_shift_right))
                link(dve.tensor_scalar(ri[:, k], ri[:, k], -1.0, MAGIC, ALU.mult, ALU.add))
                g = ri[:, k].bitcast(F32)
                for step in range(4):
                    link(dve.tensor_tensor(rt[:, k], g, g, ALU.mult))
                    link(dve.scalar_tensor_tensor(rt[:, k], rt[:, k], -0.5, ve[:, k], ALU.mult, ALU.mult))
                    link(dve.scalar_tensor_tensor(dst, rt[:, k], 1.5, g, ALU.add, ALU.mult))
                    g = dst

            def bn(src, a, b_):
                for t in range(a, b_):
                    c = link.mark(dve.bn_stats(bn6[:, t, :], src[:, t - src_at[0], :]))
                link.wait(c)
                for t in range(a, b_):
                    c = link.mark(dve.bn_aggr(mv[:, t, :], bn6[:, t, :]))
                link.wait(c)

            src_at = [0]

            def stats(a, b_):
                bn(xin, a, b_)
                rsqrt(r1[:, a:b_], mv[:, a:b_, 1], a, b_)
                link(dve.tensor_tensor(r2[:, a:b_], r1[:, a:b_], r1[:, a:b_], ALU.mult))
                link(dve.tensor_tensor(r2[:, a:b_], r2[:, a:b_], mv[:, a:b_, 1], ALU.mult))
                rsqrt(r2[:, a:b_], r2[:, a:b_], a, b_)

            def normalise(n):
                ge(dve, s("xT_ready"), n)
                for t in range(T):
                    c = link.mark(dve.tensor_scalar(x0[:, n * T + t, :], xin[:, n * T + t, :], mv[:, n * T + t, 0:1],
                                                    r1_at(n, t), ALU.subtract, ALU.mult))
                link.wait(c)
                for t in range(T):
                    i = dve.tensor_scalar(xh[:, t, :], x0[:, n * T + t, :], r2_at(n, t), None, ALU.mult)
                i.then_inc(s("xn_ready"), 1)

            def r1_at(n, t):
                return r1[:, n * T + t:n * T + t + 1] if isinstance(n, int) else r1[:, bass.ds(n * T + t, 1)]

            def r2_at(n, t):
                return r2[:, n * T + t:n * T + t + 1] if isinstance(n, int) else r2[:, bass.ds(n * T + t, 1)]

            def evac_hT(n):
                dve.wait_ge(s("xT_ready"), n + 1)
                ge(dve, s("qv_ready"), n)
                dve.tensor_scalar(hT[:, :], aux[0][:, 0:N], cols[:, 0:1], cols[:, 1:2], ALU.mult,
                                  ALU.add).then_inc(s("hT_ready"), 1)

            q_ps = aux[2][:, :].rearrange("p (t w h d) -> p w t h d", t=T, w=2, d=DH)[:, 0]

            def th(x):
                return x.rearrange("p (t h) d -> p t h d", t=T)

            def pieces_keys(n):
                dve.wait_ge(s("sq_ready"), n + 1)
                link(dve.reduce_sum(c0[:, :], sq[:, :, :].rearrange("p t (h d) -> p (t h) d", d=DH), AX_X))
                dve.tensor_tensor(cf[:, :], c0[:, :], snegb[:, :, :].rearrange("p t h -> p (t h)"),
                                  ALU.mult).then_inc(s("sum_ready"), 1)
                ge(dve, s("stT_ready"), n * 4)
                link(dve.tensor_copy(th(stackA[:, :, 0:8]), q_ps))
                link(dve.tensor_tensor(th(ra[:, :, :]), q_ps, th(stackA[:, :, 0:8]), ALU.subtract))
                link(dve.tensor_copy(stackA[:, :, 24:32], ra[:, :, :]))
                dve.tensor_tensor(stackA[:, :, 40:48], ra[:, :, :], stackA[:, :, 24:32], ALU.subtract)

            def pieces_queries(n):
                for t in range(T):
                    i = dve.tensor_tensor(pf[:, t * H:t * H + H, :], q_ps[:, t], s2b[:, :, :], ALU.mult)
                i.then_inc(s("q_read"), 1)
                dve.wait_ge(s("q_read"), n + 1)
                link(dve.tensor_copy(stackB[:, :, 0:8], pf[:, :, :]))
                link(dve.tensor_tensor(rb[:, :, :], pf[:, :, :], stackB[:, :, 0:8], ALU.subtract))
                link(dve.tensor_copy(stackB[:, :, 8:16], rb[:, :, :]))
                dve.tensor_tensor(stackB[:, :, 16:24], rb[:, :, :], stackB[:, :, 8:16],
                                  ALU.subtract).then_inc(s("pieces_ready"), 1)

            def evac_stack(n, q, k):
                bank = auxb[(2, 1, 2, 1)[k]]
                dve.wait_ge(s("stT_ready"), n * 4 + k + 1)
                if k == 0:
                    ge(dve, s("logits_ready"), n * 8 - 8)
                pr = slice(4 * (k % 2), 4 * (k % 2) + 4)
                if k < 2:
                    dve.tensor_copy(keysT[q][:, pr, :], bank.rearrange("p (j n) -> p j n", n=N))\
                       .then_inc(s("stT_read"), 1)
                else:
                    bv = bank.rearrange("p (j n) -> p j n", n=N)
                    dve.tensor_copy(qrysT[q][0:64, pr, 0, :], bv[0:64])
                    dve.tensor_copy(qrysT[q][64:128, pr, 1, :], bv[64:128]).then_inc(s("stT_read"), 1)

            def evac_pv(b, half):
                dve.wait_ge(s("pv_done"), b * 4 + 2 * half + 2)
                dve.tensor_copy(oT[:, 2 * half:2 * half + 2, :].rearrange("p g n -> p (g n)"),
                                pv_bank[:, :]).then_inc(s("o_read"), 1)

            def divide(m, half):
                bank = aux[1 - half][:, :].rearrange("p (t k c) -> p t k c", t=T, c=32)
                dve.wait_ge(s("oT_ready"), m * 2 + half + 1)
                hd = slice(8 * half, 8 * half + 8)
                link(dve.reciprocal(rden[:, :, hd], bank[:, :, :, DH]))
                dve.tensor_tensor(on[:, :, hd, :], bank[:, :, :, 0:DH],
                                  rden[:, :, hd].unsqueeze(3).broadcast_to([P, T, 8, DH]),
                                  ALU.mult).then_inc(s("on_ready"), 1)

            def residual1(m):
                dve.wait_ge(s("proj_ready"), m + 1)
                dve.tensor_tensor(tiles(x1, m), aux[0][:, 0:N].rearrange("p (t d) -> p t d", t=T), tiles(x0, m),
                                  ALU.add).then_inc(s("x1_ready"), 1)

            def tiles(x, m):
                return x[:, m * T:m * T + T, :] if isinstance(m, int) else x[:, bass.ds(m * T, T), :]

            def step(b, p):
                nxt, last = has_next(b), has_last(b)
                if nxt:
                    normalise(b + 1)
                if last:
                    evac_pv(b - 1, 1)
                if nxt:
                    evac_hT(b + 1)
                if last:
                    divide(b - 1, 0)
                if nxt:
                    pieces_keys(b + 1)
                if last:
                    divide(b - 1, 1)
                if nxt:
                    pieces_queries(b + 1)
                evac_pv(b, 0)
                if nxt:
                    evac_stack(b + 1, 1 - p, 0)
                if last:
                    residual1(b - 1)
                if nxt:
                    for k in range(1, 4):
                        evac_stack(b + 1, 1 - p, k)

            for buf in (stackA, stackB):
                dve.memset(buf[:, :, SUMCOL:SLOT], 0.0)
            for p in range(2):
                dve.memset(qrysT[p][:, :, :, :], 0.0)
                dve.memset(vaug[p][:, :, :, DH:32], 0.0)
            c = link.mark(dve.memset(rden[:, :, :], 0.0))
            link.wait(c)
            dve.memset(stackA[:, :, SUMCOL + 3:SUMCOL + 9], 1.0)
            dve.memset(stackB[:, :, SUMCOL:SUMCOL + 3], 1.0)
            for p in range(2):
                i = dve.memset(vaug[p][:, :, :, DH:DH + 1], 1.0)
            i.then_inc(s("consts_ready"), 1)
            dve.wait_ge(s("x_first"), 16)
            stats(0, T)
            normalise(0)
            dve.wait_ge(s("attn_weights"), 16 * 10)
            SCALE = float(DH) ** -0.5
            dve.tensor_scalar(s2b[:, :, :], taub[:, :].unsqueeze(2).broadcast_to([P, H, DH]), 2.0 * SCALE, None,
                              ALU.mult)
            for t in range(T):
                dve.tensor_scalar(snegb[:, t, :], taub[:, :], -SCALE, None, ALU.mult)
            link(dve.tensor_tensor(wog_t[:, :], wog_t[:, :], g1b[:, :], ALU.mult))
            evac_hT(0)
            pieces_keys(0)
            pieces_queries(0)
            for k in range(4):
                evac_stack(0, 0, k)
            dve.wait_ge(s("x_rest"), 16)
            stats(T, TILES)
            steps(dve, link, 2 * 11, step)
            m = B - 1
            evac_pv(m, 1)
            divide(m, 0)
            divide(m, 1)
            residual1(m)

            dve.wait_ge(s("chan_weights"), 16 * 6)
            dve.wait_ge(s("x1_ready"), B)
            c = link.mark(dve.tensor_scalar(cols[:, 5:6], cols[:, 4:5], 2.0 / N ** 0.5, None, ALU.mult))
            link(dve.tensor_tensor(wogc[:, :], wogc[:, :], g2b[:, :], ALU.mult))
            for g in range(2):
                a = GT * g
                bn(x1, a, a + GT)
                rsqrt(r1[:, a:a + GT], mv[:, a:a + GT, 1], a, a + GT)
                ge(dve, s("x2T_ready"), GB * g)
                ge(dve, s("tTp_ready"), GB * g)
                for t in range(GT):
                    i = dve.tensor_scalar(tn[:, t, :], x1[:, a + t, :], mv[:, a + t, 0:1], r1[:, a + t:a + t + 1],
                                          ALU.subtract, ALU.mult)
                i.then_inc(s("xn2_ready"), 1)
                for k in range(GB):
                    n = GB * g + k
                    dve.wait_ge(s("x2T_ready"), n + 1)
                    ge(dve, s("x2_ready"), GB * g)
                    dve.tensor_scalar(h2T[:, k, :], banks[2 * k][:, 0:N], cols[:, 2:3], cols[:, 3:4], ALU.mult,
                                      ALU.add).then_inc(s("h2T_ready"), 1)
                for k in range(GB):
                    n = GB * g + k
                    dve.wait_ge(s("sqc_ready"), n + 1)
                    ge(dve, s("gram_ready"), GB * g)
                    dve.tensor_copy(qc[:, k, :], banks[2 * k + 1][:, 0:T * D]).then_inc(s("qc_copied"), 1)
                for k in range(GB):
                    n = GB * g + k
                    dve.wait_ge(s("gram_ready"), n + 1)
                    ge(dve, s("at_ready"), GB * g)
                    link(dve.scalar_tensor_tensor(lg[:, k, :], banks[2 * k][:, 0:D], cols[:, 5:6], mask[:, :],
                                                  ALU.mult, ALU.add))
                    dve.tensor_reduce(nmx[:, k:k + 1], lg[:, k, :], AX_X, ALU.max, negate=True)\
                       .then_inc(s("lg_ready"), 1)
                for k in range(GB):
                    n = GB * g + k
                    dve.wait_ge(s("at_ready"), n + 1)
                    ge(dve, s("wp_ready"), GB * g)
                    link(dve.reciprocal(rsum[:, k:k + 1], ssum[:, k:k + 1]))
                    dve.tensor_scalar(atn[:, k, :], at[:, k, :], rsum[:, k:k + 1], None, ALU.mult)\
                       .then_inc(s("atn_ready"), 1)
                for k in range(GB):
                    n = GB * g + k
                    dve.wait_ge(s("wpp_ready"), n + 1)
                    ge(dve, s("x2_ready"), GB * g)
                    dve.tensor_copy(wpp[:, k, :], banks[2 * k][:, 0:D]).then_inc(s("wpp_copied"), 1)
                dve.wait_ge(s("scaled_ready"), g + 1)
                for k in range(GB):
                    n = GB * g + k
                    dve.wait_ge(s("x2_ready"), n + 1)
                    i = dve.tensor_tensor(y[:, n * T:n * T + T, :],
                                          banks[2 * k + 1][:, 0:N].rearrange("p (t d) -> p t d", t=T),
                                          xx[:, n * T:n * T + T, :], ALU.add)
                    i.then_inc(s("y_ready"), 1)
                dve.wait_ge(s("y_ready"), GB * (g + 1))
                bn(y, a, a + GT)
                rsqrt(r1[:, a:a + GT], mv[:, a:a + GT, 1], a, a + GT)
                for t in range(GT):
                    i = dve.tensor_scalar(tn[:, t, :], y[:, a + t, :], mv[:, a + t, 0:1], r1[:, a + t:a + t + 1],
                                          ALU.subtract, ALU.mult)
                i.then_inc(s("tn_ready"), 1)
                dve.wait_ge(s("rl_ready"), g + 1)
                link(dve.tensor_tensor(rl[:, a:a + GT, :], banks[1][:, 0:GT * E].rearrange("p (t e) -> p t e", e=E),
                                       swb[:, :].unsqueeze(1).broadcast_to([P, GT, E]), ALU.add))
            link(dve.tensor_reduce(rmx[:, :], rl[:, :, :], AX_X, ALU.max))
            dve.tensor_tensor(rl[:, :, :], rl[:, :, :], rmx[:, :].unsqueeze(2).broadcast_to([P, TILES, E]),
                              ALU.subtract).then_inc(s("rmx_ready"), 1)
            dve.wait_ge(s("re_ready"), 1)
            link(dve.reduce_sum(rs[:, :], re[:, :, :], AX_X))
            link(dve.reciprocal(rs[:, :], rs[:, :]))
            link(dve.tensor_reduce(rmx[:, :], re[:, :, :], AX_X, ALU.max))
            link(dve.tensor_tensor(cand[:, :, :], re[:, :, :], rmx[:, :].unsqueeze(2).broadcast_to([P, TILES, E]),
                                   ALU.is_equal))
            link(dve.tensor_scalar(iota8[:, :], iota8[:, :], float(E), None, ALU.subtract))
            link(dve.tensor_tensor(cand[:, :, :], cand[:, :, :], iota8[:, :].unsqueeze(1).broadcast_to([P, TILES, E]),
                                   ALU.mult))
            link(dve.tensor_reduce(first[:, :], cand[:, :, :], AX_X, ALU.min))
            link(dve.tensor_tensor(cand[:, :, :], first[:, :].unsqueeze(2).broadcast_to([P, TILES, E]),
                                   iota8[:, :].unsqueeze(1).broadcast_to([P, TILES, E]), ALU.is_equal))
            link(dve.tensor_tensor(rs[:, :], rs[:, :], rmx[:, :], ALU.mult))
            link(dve.tensor_tensor(pw[:, :, :], cand[:, :, :], rs[:, :].unsqueeze(2).broadcast_to([P, TILES, E]),
                                   ALU.mult))
            dve.wait_ge(s("moe_weights"), 32)
            for e in range(E):
                for c in range(4):
                    q = e * 4 + c
                    for t in range(4):
                        k = 4 * c + t
                        cc = link.mark(dve.scalar_tensor_tensor(y[:, k, :], b2b[:, e, :], pw[:, k, e:e + 1],
                                                                y[:, k, :], ALU.mult, ALU.add))
                    link.wait(cc)
                    dve.wait_ge(s("y2_ready"), q + 1)
                    for t in range(4):
                        k = 4 * c + t
                        i = dve.scalar_tensor_tensor(y[:, k, :], banks[4 + q % 2][:, t * D:t * D + D],
                                                     pw[:, k, e:e + 1], y[:, k, :], ALU.mult, ALU.add)
                    i.then_inc(s("y2_added"), 1)
                    dve.wait_ge(s("y2_added"), q + 1)

        @block.tensor
        def _(pe):
            def normT(n):
                pe.wait_ge(s("xn_ready"), n + 1)
                for t in range(T):
                    i = pe.transpose(aux[0][:, t * P:t * P + P], xh[:, t, :], ident[:, :])
                i.then_inc(s("xT_ready"), 1)

            def project_qv(n):
                pe.wait_ge(s("hT_ready"), n + 1)
                ge(pe, s("stT_read"), n * 4 - 1)
                for t in range(T):
                    i = pe.matmul(aux[2][:, t * 2 * D:(t + 1) * 2 * D], hT[:, t * P:t * P + P], wqkv[:, :],
                                  start=True, stop=True)
                i.then_inc(s("qv_ready"), 1)

            def stackT(n, k):
                if k == 0:
                    pe.wait_ge(s("stack_ready"), n + 1)
                    pe.wait_ge(s("v_ready"), n + 1)
                    pe.wait_ge(s("q_read"), n + 1)
                if k == 1:
                    ge(pe, s("onT_ready"), n - 1)
                    ge(pe, s("stT_read"), n * 4)
                if k >= 2:
                    pe.wait_ge(s("stT_read"), n * 4 + k - 1)
                bank = auxb[(2, 1, 2, 1)[k]]
                src = stackA if k < 2 else stackB
                for jj in range(4):
                    j = 4 * (k % 2) + jj
                    for t in range(T):
                        h = t * H + 2 * j
                        i = pe.transpose(bank[:, jj * N + t * P:jj * N + t * P + P],
                                         src[:, h:h + 2, :].rearrange("p h c -> p (h c)"), identb[:, :])
                i.then_inc(s("stT_ready"), 1)

            def logits(b, p, j):
                if j == 0:
                    pe.wait_ge(s("stT_read"), b * 4 + 4)
                ge(pe, s("exp_ready"), b * 8 + j - 1)
                for t in range(T):
                    i = pe.matmul(logit_banks[j % 2][t][:, :], keysT[p][:, j, t * P:t * P + P],
                                  qrysT[p][:, j, :, :].rearrange("p e n -> p (e n)"), start=True, stop=True)
                i.then_inc(s("logits_ready"), 1)

            def pv(b, p, g):
                pe.wait_ge(s("exp_ready"), b * 8 + 2 * g + 2)
                if g % 2 == 0:
                    ge(pe, s("o_read"), b * 2 + g // 2)
                for t in range(T):
                    for jj in range(4):
                        i = pe.matmul(pv_bank[32 * jj:32 * jj + 32, (g % 2) * N:(g % 2) * N + N],
                                      vaug[p][:, t, 4 * g + jj, :], expo[(2 * g + jj // 2) % 4][:, t, jj % 2, :],
                                      start=(t == 0), stop=(t == T - 1))
                i.then_inc(s("pv_done"), 1)

            def oT_back(m, half):
                pe.wait_ge(s("o_read"), m * 2 + half + 1)
                if half == 0:
                    pe.wait_ge(s("stT_read"), min(m + 2, B) * 4 if isinstance(m, int) else m * 4 + 8)
                for t in range(T):
                    for gg in range(2):
                        i = pe.transpose(aux[1 - half][:, (t * 2 + gg) * P:(t * 2 + gg) * P + P],
                                         oT[:, 2 * half + gg, t * P:t * P + P], ident[:, :])
                i.then_inc(s("oT_ready"), 1)

            def onT_(m):
                pe.wait_ge(s("on_ready"), m * 2 + 2)
                for t in range(T):
                    i = pe.transpose(aux[1][:, t * P:t * P + P], on[:, t, :, :].rearrange("p h d -> p (h d)"),
                                     ident[:, :])
                i.then_inc(s("onTp_ready"), 1)

            def project_o(m):
                pe.wait_ge(s("onT_ready"), m + 1)
                for t in range(T):
                    i = pe.matmul(aux[0][:, t * D:t * D + D], onT[:, t * P:t * P + P], wog_t[:, :], start=True,
                                  stop=True)
                i.then_inc(s("proj_ready"), 1)

            def step(b, p):
                nxt, last = has_next(b), has_last(b)
                m, n = b - 1, b + 1
                logits(b, p, 0)
                if nxt:
                    normT(n)
                if last:
                    pv(m, 1 - p, 3)
                logits(b, p, 1)
                if last:
                    oT_back(m, 0)
                if nxt:
                    project_qv(n)
                logits(b, p, 2)
                if last:
                    oT_back(m, 1)
                pv(b, p, 0)
                logits(b, p, 3)
                if last:
                    onT_(m)
                logits(b, p, 4)
                pv(b, p, 1)
                if last:
                    project_o(m)
                logits(b, p, 5)
                if nxt:
                    stackT(n, 0)
                    stackT(n, 1)
                logits(b, p, 6)
                pv(b, p, 2)
                if nxt:
                    stackT(n, 2)
                logits(b, p, 7)
                if nxt:
                    stackT(n, 3)

            pe.wait_ge(s("ident_ready"), 2)
            pe.wait_ge(s("attn_weights"), 16 * 10)
            normT(0)
            project_qv(0)
            for k in range(4):
                stackT(0, k)
            steps(pe, None, 0, step)
            m = B - 1
            pv(m, 1, 3)
            oT_back(m, 0)
            oT_back(m, 1)
            onT_(m)
            project_o(m)

            pe.wait_ge(s("chan_weights"), 16 * 6)
            pe.wait_ge(s("consts_ready"), 4)
            pe.wait_ge(s("x1_ready"), B)
            for g in range(2):
                pe.wait_ge(s("xn2_ready"), g + 1)
                for k in range(GB):
                    for t in range(T):
                        i = pe.transpose(banks[2 * k][:, t * P:t * P + P], tn[:, k * T + t, :], ident[:, :])
                    i.then_inc(s("x2T_ready"), 1)
                for k in range(GB):
                    pe.wait_ge(s("h2T_ready"), GB * g + k + 1)
                    for t in range(T):
                        i = pe.matmul(banks[2 * k + 1][:, t * D:t * D + D], h2T[:, k, t * P:t * P + P], wqkc[:, :],
                                      start=True, stop=True)
                    i.then_inc(s("qc_ready"), 1)
                for k in range(GB):
                    pe.wait_ge(s("qc_copied"), GB * g + k + 1)
                    o = banks[2 * k][:, 0:D]
                    for t in range(T):
                        q_, q2_ = qc[:, k, t * D:t * D + D], sqc[:, k, t * D:t * D + D]
                        pe.matmul(o, q_, q_, start=(t == 0), stop=False)
                        pe.matmul(o, nhalf[:, :], q2_, start=False, stop=False)
                        i = pe.matmul(o, q2_, nhalf[:, :], start=False, stop=(t == T - 1))
                    i.then_inc(s("gram_ready"), 1)
                for k in range(GB):
                    pe.wait_ge(s("atn_ready"), GB * g + k + 1)
                    pe.matmul(banks[2 * k + 1][:, 0:D], atn[:, k, :], wogc[:, :], start=True, stop=True)\
                      .then_inc(s("wp_ready"), 1)
                for k in range(GB):
                    pe.wait_ge(s("wp_copied"), GB * g + k + 1)
                    pe.matmul(banks[2 * k][:, 0:D], wvTc[:, :], wp[:, k, :], start=True, stop=True)\
                      .then_inc(s("wpp_ready"), 1)
                for k in range(GB):
                    pe.wait_ge(s("wpp_copied"), GB * g + k + 1)
                    for t in range(T):
                        i = pe.matmul(banks[2 * k + 1][:, t * D:t * D + D], h2T[:, k, t * P:t * P + P], wpp[:, k, :],
                                      start=True, stop=True)
                    i.then_inc(s("x2_ready"), 1)
                pe.wait_ge(s("tn_ready"), g + 1)
                for k in range(GB):
                    for t in range(T):
                        i = pe.transpose(banks[2 * k][:, t * P:t * P + P], tn[:, k * T + t, :], ident[:, :])
                    i.then_inc(s("tTp_ready"), 1)
                for k in range(GB):
                    pe.wait_ge(s("tT_ready"), GB * g + k + 1)
                    for t in range(T):
                        at_ = (GB * g + k) * N + t * P
                        i = pe.matmul(banks[1][:, (k * T + t) * E:(k * T + t) * E + E], tT[:, at_:at_ + P], sww[:, :],
                                      start=True, stop=True)
                i.then_inc(s("rl_ready"), 1)

            def layer1(e, c):
                q = e * 4 + c
                for f in range(FT):
                    ge(pe, s("gelu_ready"), (q - 1) * FT + f + 1)
                    pe.matmul(banks[f][:, :], w1b[e % 2][:, f * P:f * P + P], tT[:, c * 512:c * 512 + 512], start=True,
                              stop=True).then_inc(s("h_ready"), 1)

            def layer2(e, c):
                q = e * 4 + c
                pe.wait_ge(s("gelu_ready"), q * FT + FT)
                ge(pe, s("y2_added"), q - 1)
                for t in range(4):
                    for f in range(FT):
                        i = pe.matmul(banks[4 + q % 2][:, t * D:t * D + D], hsb[q % 2][:, f, t * P:t * P + P],
                                      w2b[e % 2][:, f, :], start=(f == 0), stop=(f == FT - 1))
                i.then_inc(s("y2_ready"), 1)

            pe.wait_ge(s("rmx_ready"), 1)
            for q in range(E * 4 + 1):
                if q < E * 4:
                    if q % 4 == 0:
                        pe.wait_ge(s(f"ew_loaded{q // 4 % 2}"), 32 * (q // 8 + 1))
                    layer1(q // 4, q % 4)
                if q:
                    layer2((q - 1) // 4, (q - 1) % 4)


def kernel(**inputs):
    import numpy as _np
    import concourse.bacc as _bacc
    from concourse import mybir as _mybir
    from concourse.bass_utils import run_bass_kernel_spmd as _run

    a = {k.split("_", 2)[2]: _np.asarray(v) for k, v in inputs.items()}
    col = lambda v: v.reshape(-1, 1)
    laid = [
        ("x", a["x"]), ("wqk_t", a["Wqk_t"]), ("wv_t", a["Wv_t"]), ("wo_t", a["Wo_t"]), ("tau_t", a["tau_t"].reshape(-1)),
        ("wqk_c", a["Wqk_c"]), ("wvT_c", a["Wv_c"].T), ("wo_c", a["Wo_c"]),
        ("tau_c", col(_np.repeat(a["tau_c"].reshape(-1), CDH))),
        ("ln1_w", col(a["ln1_w"])), ("ln1_b", col(a["ln1_b"])), ("ln2_w", col(a["ln2_w"])), ("ln2_b", col(a["ln2_b"])),
        ("gamma1", a["gamma1"]), ("gamma2", a["gamma2"]), ("switch_w", a["switch_w"]), ("switch_b", a["switch_b"]),
        ("w1", a["w1"]), ("b1T", a["b1"].reshape(E * FT, P).T), ("w2", a["w2"]), ("b2", a["b2"]),
    ]
    nc = _bacc.Bacc("TRN2", target_bir_lowering=False, num_devices=1)
    arrays, args = {}, []
    for name, v in laid:
        v = _np.ascontiguousarray(v)
        arrays[f"in_{name}"] = v
        args.append(nc.dram_tensor(f"in_{name}", v.shape, _mybir.dt.from_np(v.dtype), kind="ExternalInput").ap())
    args.append(nc.dram_tensor("out_0", (B, N, D), F32, kind="ExternalOutput").ap())
    build(nc, *args)
    r = _run(nc, [arrays], core_ids=[0])
    return r.results[0]["out_0"]
```

```python
from contextlib import ExitStack

import concourse.bass as bass
from concourse import mybir

P = 128
F32 = mybir.dt.float32
BF16 = mybir.dt.bfloat16
I32 = mybir.dt.int32
ALU = mybir.AluOpType
ACT = mybir.ActivationFunctionType
AX_X = mybir.AxisListType.X

EPS = 1e-5
B, N, D = 8, 256, 128
H, DH = 16, 8
CH, CDH = 8, 16
E, F = 8, 512
T = N // P
TILES = B * T
PAIRS = H // 2
GROUPS = H // 4
SLOT = 64
PIECES = 3
SUMCOL = 6 * DH
NEG = -1.0e30
FT = F // P
REGION = B * N + P
NSLOT = E * REGION + P
REC = 2 * D + 2
PROB, IDENT = 2 * D, 2 * D + 1
RING = 4
JT = -(-((B * N + E * (P - 1)) // P) // RING) * RING
NOBODY = 4095
MAGIC = float(0x5F3759DF)


class Link:

    def __init__(self, eng, sem):
        self.eng, self.sem, self.n, self.turn, self.per = eng, sem, 0, None, 0

    def loop(self, i, per):
        self.turn, self.per, self.at = i, per, self.n

    def end(self, turns):
        assert self.n - self.at == self.per, self.n - self.at
        self.n, self.turn = self.at + self.per * turns, None

    def value(self):
        return self.n if self.turn is None else self.turn * self.per + self.n

    def mark(self, ins):
        ins.then_inc(self.sem, 1)
        self.n += 1
        return self.value()

    def wait(self, value):
        self.eng.wait_ge(self.sem, value)

    def __call__(self, ins):
        self.wait(self.mark(ins))


def ge(eng, sem, value):
    if not isinstance(value, int) or value > 0:
        eng.wait_ge(sem, value)


def build(nc, x_in, wqk_t, wv_t, wo_t, tau_t, wqk_c, wvT_c, wo_c, tau_c, ln1_w, ln1_b, ln2_w, ln2_b,
          gamma1, gamma2, switch_w, switch_b, w1, b1T, w2, b2, out):
    with ExitStack() as ctx:
        def sb(name, shape, dt=F32):
            return ctx.enter_context(nc.sbuf_tensor(name, shape, dt))

        def sem(name):
            return ctx.enter_context(nc.semaphore(name))

        psum = ctx.enter_context(nc.psum_tensor("psum", [P, 8, 512], F32))
        banks = [psum[:, i, :] for i in range(8)]
        logit_banks = [banks[0:2], banks[2:4]]
        pv_bank = banks[4]
        aux = banks[5:8]
        auxb = [a.bitcast(BF16) for a in aux]

        xin = sb("xin", [P, TILES, D])
        x0 = sb("x0", [P, TILES, D])
        x1 = sb("x1", [P, TILES, D])
        ident = sb("ident", [P, P])
        identb = sb("identb", [P, P], BF16)
        bn6 = sb("bn6", [P, TILES, 6])
        mv = sb("mv", [P, TILES, 2])
        ve = sb("ve", [P, TILES])
        ri = sb("ri", [P, TILES], I32)
        rt = sb("rt", [P, TILES])
        r1 = sb("r1", [P, TILES])
        r2 = sb("r2", [P, TILES])
        wqkv = sb("wqkv", [P, 2 * D])
        wog_t = sb("wog_t", [P, D])
        g1b = sb("g1b", [P, D])
        cols = sb("cols", [P, 8])
        taub = sb("taub", [P, H])
        s2b = sb("s2b", [P, H, DH])
        snegb = sb("snegb", [P, T, H])
        xh = sb("xh", [P, T, D])
        hT = sb("hT", [P, N])
        sq = sb("sq", [P, T, D])
        ra = sb("ra", [P, T * H, DH])
        pf = sb("pf", [P, T * H, DH])
        rb = sb("rb", [P, T * H, DH])
        c0 = sb("c0", [P, T * H])
        cf = sb("cf", [P, T * H])
        rc = sb("rc", [P, T * H])
        ones = sb("ones", [P, T * H])
        stackA = sb("stackA", [P, T * H, SLOT], BF16)
        stackB = sb("stackB", [P, T * H, SLOT], BF16)
        keysT = [sb(f"keysT{p}", [P, PAIRS, N], BF16) for p in range(2)]
        qrysT = [sb(f"qrysT{p}", [P, PAIRS, 2, N], BF16) for p in range(2)]
        vaug = [sb(f"vaug{p}", [P, T, H, 32]) for p in range(2)]
        expo_all = sb("expo_all", [P, 4 * T * 2 * N])
        expo = [expo_all[:, i * T * 2 * N:(i + 1) * T * 2 * N].rearrange("p (t e n) -> p t e n", t=T, e=2)
                for i in range(4)]
        oT = sb("oT", [P, GROUPS, N])
        rden = sb("rden", [P, T, H])
        on = sb("on", [P, T, H, DH])
        onT = sb("onT", [P, N])
        wqkc = sb("wqkc", [P, D])
        wvTc = sb("wvTc", [P, D])
        wogc = sb("wogc", [P, D])
        g2b = sb("g2b", [P, D])
        mask = sb("mask", [P, D])
        nhalf = sb("nhalf", [P, D])
        GB = 4
        GT = GB * T
        h2T = sb("h2T", [P, GB, N])
        qc = sb("qc", [P, GB, T * D])
        sqc = sb("sqc", [P, GB, T * D])
        lg = sb("lg", [P, GB, D])
        nmx = sb("nmx", [P, GB])
        ssum = sb("ssum", [P, GB])
        rsum = sb("rsum", [P, GB])
        at = sb("at", [P, GB, D])
        atn = sb("atn", [P, GB, D])
        wp = sb("wp", [P, GB, D])
        wpp = sb("wpp", [P, GB, D])
        rec = sb("rec", [P, TILES, REC])
        tn = sb("tn", [P, GT, D])
        tT = sb("tT", [P, GB, N])
        sww = sb("sww", [P, E])
        swb = sb("swb", [P, E])
        rl = sb("rl", [P, GT, E])
        rmx = sb("rmx", [P, GT])
        re = sb("re", [P, GT, E])
        rs = sb("rs", [P, GT])
        iota8 = sb("iota8", [P, E])
        ebase = sb("ebase", [P, E])
        minus8 = sb("minus8", [P, E])
        jiota = sb("jiota", [P, JT])
        cand = sb("cand", [P, GT, E])
        first = sb("first", [P, GT])
        oh = sb("oh", [P, 1 + TILES, E], BF16)
        before = sb("before", [P, P], BF16)
        onesb = sb("onesb", [P, P], BF16)
        rank = sb("rank", [P, GT, E])
        pos = sb("pos", [P, TILES], I32)
        ones8 = sb("ones8", [P, E])
        cnt_i = sb("cnt_i", [P, E], I32)
        ntile = sb("ntile", [P, E])
        cum = sb("cum", [P, E])
        past = sb("past", [P, JT, E])
        ej = sb("ej", [P, JT])
        rj = sb("rj", [P, JT])
        etab = sb("etab", [P, JT], I32)
        rtab = sb("rtab", [P, JT], I32)
        ptab = sb("ptab", [P, E], I32)
        padrec = sb("padrec", [P, REC])
        b1s = sb("b1s", [P, E, FT])
        b2b = sb("b2b", [P, E, D])
        w2s = sb("w2s", [P, E, FT, D])
        w1j = [sb(f"w1j{i}", [P, F]) for i in range(RING)]
        tj = [sb(f"tj{i}", [P, D]) for i in range(RING)]
        yj = sb("yj", [P, JT, REC - D])
        tTj = [sb(f"tTj{i}", [P, P]) for i in range(2)]
        hpre = [sb(f"hpre{i}", [P, FT, P]) for i in range(2)]
        hj = [sb(f"hj{i}", [P, FT, P]) for i in range(2)]
        zj = [sb(f"zj{i}", [P, D]) for i in range(2)]
        oj = expo_all[:, 0:JT * D].rearrange("p (j d) -> p j d", d=D)
        slots = nc.dram_tensor("slots", (NSLOT, REC), F32).ap()

        S = {}

        def s(name):
            if name not in S:
                S[name] = sem(name)
            return S[name]

        for name in ("x_first x_rest attn_weights chan_weights moe_weights ident_ready consts_ready pool_link dve_link zj_ready "
                     "act_link xn_ready xT_ready hT_ready qv_ready v_ready sq_ready q_read sum_ready "
                     "sums_ready stack_ready stT_ready stT_read logits_ready exp_ready pv_done o_read oT_ready on_ready "
                     "onTp_ready onT_ready proj_ready x1_ready scaled_ready "
                     "xn2_ready x2T_ready h2T_ready qc_ready qc_copied sqc_ready gram_ready lg_ready at_ready atn_ready "
                     "wp_ready wp_copied wpp_ready wpp_copied x2_ready y_ready tn_ready tTp_ready tT_ready rl_ready "
                     "rmx_ready re_ready oh_ready rank_ready pos_ready ids_ready pad_ready table_ready sorted padded "
                     "tj_ready tTj_ready h_ready hpre_ready gelu_ready z_ready o_ready tj_loaded0 tj_loaded1 "
                     "tj_loaded2 tj_loaded3 yj_loaded0 yj_loaded1 yj_loaded2 yj_loaded3 w1_loaded0 w1_loaded1 w1_loaded2 w1_loaded3 out_written").split():
            s(name)

        block = ctx.enter_context(nc.Block())

        def steps(eng, link, per, step):
            step(0, 0)
            if eng is not None:
                with eng.Fori(0, (B - 2) // 2) as i:
                    if link:
                        link.loop(i, per)
                    step(i * 2 + 1, 1)
                    step(i * 2 + 2, 0)
                if link:
                    link.end((B - 2) // 2)
            step(B - 1, 1)

        def col_at(table, j):
            return table[0:1, j:j + 1] if isinstance(j, int) else table[0:1, bass.ds(j, 1)]

        def at_j(x, j):
            return x[:, j, :] if isinstance(j, int) else x[:, bass.ds(j, 1), :].rearrange("p a d -> p (a d)")

        def tiles_of_experts(eng, step):
            for k in range(RING):
                step(k, k, 0)
            with eng.Fori(1, JT // RING - 1) as j4:
                for k in range(RING):
                    step(j4 * RING + k, k, j4)
            for k in range(RING):
                step(JT - RING + k, k, JT // RING - 1)

        def ahead(j, n):
            return not isinstance(j, int) or j + n < JT

        has_next = lambda b: not isinstance(b, int) or b + 1 < B
        has_last = lambda b: not isinstance(b, int) or b > 0

        @block.sync
        def _(sp):
            xv = x_in.rearrange("b (t p) d -> p (b t) d", p=P)
            sp.dma_start(xin[:, 0:T, :], xv[:, 0:T, :]).then_inc(s("x_first"), 16)
            sp.dma_start(wqkv[:, 0:D], wqk_t).then_inc(s("attn_weights"), 16)
            sp.dma_start(wqkv[:, D:2 * D], wv_t).then_inc(s("attn_weights"), 16)
            for k, v in enumerate((ln1_w, ln1_b, ln2_w, ln2_b, tau_c)):
                sp.dma_start(cols[:, k:k + 1], v).then_inc(s("attn_weights"), 16)
            sp.dma_start(taub[:, :], tau_t.partition_broadcast(P)).then_inc(s("attn_weights"), 16)
            sp.dma_start(g1b[:, :], gamma1.partition_broadcast(P)).then_inc(s("attn_weights"), 16)
            sp.dma_start(wog_t[:, :], wo_t).then_inc(s("attn_weights"), 16)
            sp.dma_start(xin[:, T:, :], xv[:, T:, :]).then_inc(s("x_rest"), 16)
            sp.dma_start(wqkc[:, :], wqk_c).then_inc(s("chan_weights"), 16)
            sp.dma_start(wvTc[:, :], wvT_c).then_inc(s("chan_weights"), 16)
            sp.dma_start(wogc[:, :], wo_c).then_inc(s("chan_weights"), 16)
            sp.dma_start(g2b[:, :], gamma2.partition_broadcast(P)).then_inc(s("chan_weights"), 16)
            sp.dma_start(sww[:, :], switch_w).then_inc(s("chan_weights"), 16)
            sp.dma_start(swb[:, :], switch_b.partition_broadcast(P)).then_inc(s("chan_weights"), 16)
            sp.dma_start(b1s[:, :], b1T).then_inc(s("moe_weights"), 16)
            sp.dma_start(b2b[:, :, :].rearrange("p e d -> p (e d)"),
                         b2.rearrange("e d -> (e d)").partition_broadcast(P)).then_inc(s("moe_weights"), 16)
            w2v = w2.rearrange("e (t p) d -> p e t d", p=P)
            for e in range(E):
                sp.dma_start(w2s[:, e, :, :], w2v[:, e, :, :]).then_inc(s("moe_weights"), 16)
            sp.wait_ge(s("pad_ready"), 2)
            sp.dma_start(slots[E * REGION:NSLOT, :], padrec[:, :]).then_inc(s("padded"), 16)
            sp.wait_ge(s("table_ready"), 1)
            for e in range(E):
                row = sp.value_load(ptab[0:1, e:e + 1], min_val=e * REGION, max_val=e * REGION + B * N)
                sp.dma_start(slots[bass.ds(row, P), :], padrec[:, :]).then_inc(s("padded"), 16)
            sp.wait_ge(s("sorted"), TILES * 16)
            sp.wait_ge(s("padded"), (E + 1) * 16)

            def load(j, k, first=False):
                ex = sp.value_load(col_at(etab, j), min_val=0, max_val=E - 1)
                row = sp.value_load(col_at(rtab, j), min_val=0, max_val=NSLOT - P)
                if not first:
                    sp.wait_ge(s("h_ready"), j - RING + 1)
                sp.dma_start(tj[k][:, :], slots[bass.ds(row, P), 0:D]).then_inc(s(f"tj_loaded{k}"), 16)
                sp.dma_start(w1j[k][:, :], w1[bass.ds(ex, 1), :, :].rearrange("e d f -> (e d) f"))\
                  .then_inc(s(f"w1_loaded{k}"), 16)
                sp.dma_start(at_j(yj, j), slots[bass.ds(row, P), D:REC]).then_inc(s(f"yj_loaded{k}"), 16)

            for k in range(RING):
                load(k, k, True)
            with sp.Fori(1, JT // RING) as j4:
                for k in range(RING):
                    load(j4 * RING + k, k)
            sp.wait_ge(s("out_written"), JT * 16)

        @block.gpsimd
        def _(pool):
            link = Link(pool, s("pool_link"))
            pool.memset(ident[:, :], 0.0).then_inc(s("pool_link"), 1)
            pool.memset(identb[:, :], 0.0).then_inc(s("pool_link"), 1)
            link.n = 2
            link.wait(2)
            for m in (ident, identb):
                pool.affine_select(out=m[:, :], in_=m[:, :], compare_op=ALU.not_equal, fill=1.0, base=0,
                                   pattern=[[-1, P]], channel_multiplier=1).then_inc(s("ident_ready"), 1)
            link(pool.memset(ones[:, :], 1.0))
            pool.memset(nhalf[:, :], -0.5).then_inc(s("consts_ready"), 1)
            link(pool.memset(mask[:, :], 0.0))
            mv3 = mask[:, :].rearrange("p (k c) -> p k c", c=CDH)
            link(pool.affine_select(out=mv3, in_=mv3, compare_op=ALU.is_ge, fill=NEG, base=0,
                                    pattern=[[-CDH, CH], [0, CDH]], channel_multiplier=1))
            pool.affine_select(out=mv3, in_=mv3, compare_op=ALU.is_ge, fill=NEG, base=CDH - 1,
                               pattern=[[CDH, CH], [0, CDH]], channel_multiplier=-1).then_inc(s("consts_ready"), 1)
            for row, step_, size in ((iota8, 1, E), (ebase, REGION, E), (jiota, 1, JT)):
                pool.iota(row[:, :], pattern=[[step_, size]], base=0, channel_multiplier=0,
                          allow_small_or_imprecise_dtypes=True).then_inc(s("consts_ready"), 1)
            pool.iota(rec[:, :, IDENT].bitcast(I32), pattern=[[P, TILES]], base=0, channel_multiplier=1)\
                .then_inc(s("ids_ready"), 1)
            link(pool.memset(before[:, :], 1.0))
            pool.affine_select(out=before[:, :], in_=before[:, :], compare_op=ALU.is_ge, fill=0.0, base=-1,
                               pattern=[[1, P]], channel_multiplier=-1).then_inc(s("consts_ready"), 1)
            pool.memset(onesb[:, :], 1.0).then_inc(s("consts_ready"), 1)
            pool.memset(ones8[:, :], 1.0).then_inc(s("consts_ready"), 1)
            pool.memset(padrec[:, 0:IDENT], 0.0).then_inc(s("pad_ready"), 1)
            pool.memset(padrec[:, IDENT:REC].bitcast(I32), NOBODY).then_inc(s("pad_ready"), 1)

            def copy(dst, src):
                return pool.tensor_tensor(dst, src, ones[:, :].unsqueeze(2).broadcast_to([P, T * H, src.shape[2]]), ALU.mult)

            def sum_pieces(n):
                pool.wait_ge(s("sum_ready"), n + 1)
                ge(pool, s("stT_ready"), n * 4)
                link(copy(stackA[:, :, SUMCOL:SUMCOL + 1], cf[:, :].unsqueeze(2)))
                link(pool.tensor_tensor(rc[:, :].unsqueeze(2), cf[:, :].unsqueeze(2),
                                        stackA[:, :, SUMCOL:SUMCOL + 1], ALU.subtract))
                link(copy(stackA[:, :, SUMCOL + 1:SUMCOL + 2], rc[:, :].unsqueeze(2)))
                link(pool.tensor_tensor(stackA[:, :, SUMCOL + 2:SUMCOL + 3], rc[:, :].unsqueeze(2),
                                        stackA[:, :, SUMCOL + 1:SUMCOL + 2], ALU.subtract))
                copy(stackB[:, :, SUMCOL + 3:SUMCOL + 6], stackA[:, :, SUMCOL:SUMCOL + 3])\
                    .then_inc(s("sums_ready"), 1)

            sum_pieces(0)
            steps(pool, link, 8, lambda b, p: sum_pieces(b + 1) if has_next(b) else None)
            for g in range(2):
                pool.wait_ge(s("x1_ready"), GB * g + GB)
                pool.tensor_tensor(xin[:, GT * g:GT * g + GT, :], x1[:, GT * g:GT * g + GT, :],
                                   xin[:, GT * g:GT * g + GT, :], ALU.add).then_inc(s("scaled_ready"), 1)
            pool.wait_ge(s("ids_ready"), 1)
            for g in range(2):
                pool.wait_ge(s("pos_ready"), g + 1)
                for k in range(GT * g, GT * g + GT):
                    pool.indirect_dma_start(slots[:, :], bass.IndirectOffsetOnAxis(ap=pos[:, k:k + 1], axis=0),
                                            rec[:, k, :], None).then_inc(s("sorted"), 16)

            out_rows = out.rearrange("b n d -> (b n) d")

            last_row = pool.to_reg(B * N - 1)

            def send(j, k):
                pool.wait_ge(s("o_ready"), j + 1)
                pool.indirect_dma_start(out_rows, bass.IndirectOffsetOnAxis(ap=yj[:, j, IDENT - D:].bitcast(I32), axis=0),
                                        oj[:, j, :], None, bounds_check=last_row, oob_is_err=False)\
                    .then_inc(s("out_written"), 16)

            for j in range(JT):
                send(j, j % RING)

        @block.scalar
        def _(act):
            def evac_v(n, q):
                act.wait_ge(s("qv_ready"), n + 1)
                ge(act, s("pv_done"), n * 4 - 4)
                act.activation(vaug[q][:, :, :, 0:DH],
                               aux[2][:, :].rearrange("p (t w h d) -> p w t h d", t=T, w=2, d=DH)[:, 1],
                               ACT.Copy).then_inc(s("v_ready"), 1)
                ge(act, s("sum_ready"), n)
                act.activation(sq[:, :, :], aux[2][:, :].rearrange("p (t w) -> p t w", t=T)[:, :, 0:D],
                               ACT.Square).then_inc(s("sq_ready"), 1)

            def exps(b, j):
                act.wait_ge(s("logits_ready"), b * 8 + j + 1)
                ge(act, s("pv_done"), b * 4 + (j - 4) // 2 + 1)
                act.activation(expo[j % 4][:, :, :, :].rearrange("p t e n -> p t (e n)"),
                               lg_view(j % 2), ACT.Exp).then_inc(s("exp_ready"), 1)

            def lg_view(k):
                return psum[:, 2 * k:2 * k + 2, :]

            def evac_onT(m):
                act.wait_ge(s("onTp_ready"), m + 1)
                act.activation(onT[:, :], aux[1][:, 0:N], ACT.Copy).then_inc(s("onT_ready"), 1)

            def step(b, p):
                for j in range(8):
                    exps(b, j)
                    if j == 1 and has_next(b):
                        evac_v(b + 1, 1 - p)
                    if j == 3 and has_last(b):
                        evac_onT(b - 1)

            act.wait_ge(s("consts_ready"), 9)
            evac_v(0, 0)
            steps(act, None, 0, step)
            evac_onT(B - 1)

            for g in range(2):
                for k in range(GB):
                    act.wait_ge(s("qc_ready"), GB * g + k + 1)
                    ge(act, s("gram_ready"), GB * g)
                    act.activation(sqc[:, k, :], banks[2 * k + 1][:, 0:T * D], ACT.Square).then_inc(s("sqc_ready"), 1)
                for k in range(GB):
                    act.wait_ge(s("lg_ready"), GB * g + k + 1)
                    ge(act, s("atn_ready"), GB * g)
                    act.activation(at[:, k, :], lg[:, k, :], ACT.Exp, bias=nmx[:, k:k + 1],
                                   accum_out=ssum[:, k:k + 1]).then_inc(s("at_ready"), 1)
                for k in range(GB):
                    act.wait_ge(s("wp_ready"), GB * g + k + 1)
                    ge(act, s("wpp_ready"), GB * g)
                    act.activation(wp[:, k, :], banks[2 * k + 1][:, 0:D], ACT.Copy).then_inc(s("wp_copied"), 1)
                for k in range(GB):
                    act.wait_ge(s("tTp_ready"), GB * g + k + 1)
                    ge(act, s("rl_ready"), g)
                    act.activation(tT[:, k, :], banks[2 * k][:, 0:N], ACT.Copy).then_inc(s("tT_ready"), 1)
                act.wait_ge(s("rmx_ready"), g + 1)
                act.activation(re[:, :, :], rl[:, :, :], ACT.Exp).then_inc(s("re_ready"), 1)

            def copy_tT(j, k):
                act.wait_ge(s("tj_ready"), j + 1)
                ge(act, s("h_ready"), j - 1)
                act.activation(tTj[k % 2][:, :], banks[k % 2][:, 0:P], ACT.Copy).then_inc(s("tTj_ready"), 1)

            def gelu(j, k):
                act.wait_ge(s("hpre_ready"), j + 1)
                ge(act, s("z_ready"), j - 1)
                act.activation(hj[k % 2][:, :, :], hpre[k % 2][:, :, :], ACT.Gelu_apprx_tanh)\
                   .then_inc(s("gelu_ready"), 1)

            copy_tT(0, 0)
            copy_tT(1, 1)
            gelu(0, 0)

            def step(j, k, turn):
                if ahead(j, 2):
                    copy_tT(j + 2, k)
                if ahead(j, 1):
                    gelu(j + 1, k + 1)

            tiles_of_experts(act, step)

        @block.vector
        def _(dve):
            link = Link(dve, s("dve_link"))

            def rsqrt(dst, v, a, b_, eps=EPS):
                k = slice(a, b_)
                link(dve.tensor_scalar(ve[:, k], v, eps, None, ALU.add))
                link(dve.tensor_scalar(ri[:, k], ve[:, k].bitcast(I32), 1, None, ALU.arith_shift_right))
                link(dve.tensor_scalar(ri[:, k], ri[:, k], -1.0, MAGIC, ALU.mult, ALU.add))
                g = ri[:, k].bitcast(F32)
                for step in range(4):
                    link(dve.tensor_tensor(rt[:, k], g, g, ALU.mult))
                    link(dve.scalar_tensor_tensor(rt[:, k], rt[:, k], -0.5, ve[:, k], ALU.mult, ALU.mult))
                    link(dve.scalar_tensor_tensor(dst, rt[:, k], 1.5, g, ALU.add, ALU.mult))
                    g = dst

            def bn(src, a, b_):
                for t in range(a, b_):
                    c = link.mark(dve.bn_stats(bn6[:, t, :], src[:, t - src_at[0], :]))
                link.wait(c)
                for t in range(a, b_):
                    c = link.mark(dve.bn_aggr(mv[:, t, :], bn6[:, t, :]))
                link.wait(c)

            src_at = [0]

            def stats(a, b_):
                bn(xin, a, b_)
                rsqrt(r1[:, a:b_], mv[:, a:b_, 1], a, b_)
                link(dve.tensor_tensor(r2[:, a:b_], r1[:, a:b_], r1[:, a:b_], ALU.mult))
                link(dve.tensor_tensor(r2[:, a:b_], r2[:, a:b_], mv[:, a:b_, 1], ALU.mult))
                rsqrt(r2[:, a:b_], r2[:, a:b_], a, b_)

            def normalise(n):
                ge(dve, s("xT_ready"), n)
                for t in range(T):
                    c = link.mark(dve.tensor_scalar(x0[:, n * T + t, :], xin[:, n * T + t, :], mv[:, n * T + t, 0:1],
                                                    r1_at(n, t), ALU.subtract, ALU.mult))
                link.wait(c)
                for t in range(T):
                    i = dve.tensor_scalar(xh[:, t, :], x0[:, n * T + t, :], r2_at(n, t), None, ALU.mult)
                i.then_inc(s("xn_ready"), 1)

            def r1_at(n, t):
                return r1[:, n * T + t:n * T + t + 1] if isinstance(n, int) else r1[:, bass.ds(n * T + t, 1)]

            def r2_at(n, t):
                return r2[:, n * T + t:n * T + t + 1] if isinstance(n, int) else r2[:, bass.ds(n * T + t, 1)]

            def evac_hT(n):
                dve.wait_ge(s("xT_ready"), n + 1)
                ge(dve, s("qv_ready"), n)
                dve.tensor_scalar(hT[:, :], aux[0][:, 0:N], cols[:, 0:1], cols[:, 1:2], ALU.mult,
                                  ALU.add).then_inc(s("hT_ready"), 1)

            q_ps = aux[2][:, :].rearrange("p (t w h d) -> p w t h d", t=T, w=2, d=DH)[:, 0]

            def th(x):
                return x.rearrange("p (t h) d -> p t h d", t=T)

            def pieces_keys(n):
                dve.wait_ge(s("sq_ready"), n + 1)
                link(dve.reduce_sum(c0[:, :], sq[:, :, :].rearrange("p t (h d) -> p (t h) d", d=DH), AX_X))
                dve.tensor_tensor(cf[:, :], c0[:, :], snegb[:, :, :].rearrange("p t h -> p (t h)"),
                                  ALU.mult).then_inc(s("sum_ready"), 1)
                ge(dve, s("stT_ready"), n * 4)
                link(dve.tensor_copy(th(stackA[:, :, 0:8]), q_ps))
                link(dve.tensor_tensor(th(ra[:, :, :]), q_ps, th(stackA[:, :, 0:8]), ALU.subtract))
                link(dve.tensor_copy(stackA[:, :, 24:32], ra[:, :, :]))
                dve.tensor_tensor(stackA[:, :, 40:48], ra[:, :, :], stackA[:, :, 24:32], ALU.subtract)
                dve.tensor_copy(stackA[:, :, 8:24].rearrange("p k (r d) -> p k r d", d=8),
                                stackA[:, :, 0:8].unsqueeze(2).broadcast_to([P, T * H, 2, 8]))
                dve.tensor_copy(stackA[:, :, 32:40], stackA[:, :, 24:32])

            def pieces_queries(n):
                for t in range(T):
                    i = dve.tensor_tensor(pf[:, t * H:t * H + H, :], q_ps[:, t], s2b[:, :, :], ALU.mult)
                i.then_inc(s("q_read"), 1)
                dve.wait_ge(s("q_read"), n + 1)
                link(dve.tensor_copy(stackB[:, :, 0:8], pf[:, :, :]))
                link(dve.tensor_tensor(rb[:, :, :], pf[:, :, :], stackB[:, :, 0:8], ALU.subtract))
                link(dve.tensor_copy(stackB[:, :, 8:16], rb[:, :, :]))
                dve.tensor_tensor(stackB[:, :, 16:24], rb[:, :, :], stackB[:, :, 8:16], ALU.subtract)
                dve.tensor_copy(stackB[:, :, 24:40], stackB[:, :, 0:16])
                dve.tensor_copy(stackB[:, :, 40:48], stackB[:, :, 0:8]).then_inc(s("stack_ready"), 1)

            def evac_stack(n, q, k):
                bank = auxb[(2, 1, 2, 1)[k]]
                dve.wait_ge(s("stT_ready"), n * 4 + k + 1)
                if k == 0:
                    ge(dve, s("logits_ready"), n * 8 - 8)
                pr = slice(4 * (k % 2), 4 * (k % 2) + 4)
                if k < 2:
                    dve.tensor_copy(keysT[q][:, pr, :], bank.rearrange("p (j n) -> p j n", n=N))\
                       .then_inc(s("stT_read"), 1)
                else:
                    bv = bank.rearrange("p (j n) -> p j n", n=N)
                    dve.tensor_copy(qrysT[q][0:64, pr, 0, :], bv[0:64])
                    dve.tensor_copy(qrysT[q][64:128, pr, 1, :], bv[64:128]).then_inc(s("stT_read"), 1)

            def evac_pv(b, half):
                dve.wait_ge(s("pv_done"), b * 4 + 2 * half + 2)
                dve.tensor_copy(oT[:, 2 * half:2 * half + 2, :].rearrange("p g n -> p (g n)"),
                                pv_bank[:, :]).then_inc(s("o_read"), 1)

            def divide(m, half):
                bank = aux[1 - half][:, :].rearrange("p (t k c) -> p t k c", t=T, c=32)
                dve.wait_ge(s("oT_ready"), m * 2 + half + 1)
                hd = slice(8 * half, 8 * half + 8)
                link(dve.reciprocal(rden[:, :, hd], bank[:, :, :, DH]))
                dve.tensor_tensor(on[:, :, hd, :], bank[:, :, :, 0:DH],
                                  rden[:, :, hd].unsqueeze(3).broadcast_to([P, T, 8, DH]),
                                  ALU.mult).then_inc(s("on_ready"), 1)

            def residual1(m):
                dve.wait_ge(s("proj_ready"), m + 1)
                dve.tensor_tensor(tiles(x1, m), aux[0][:, 0:N].rearrange("p (t d) -> p t d", t=T), tiles(x0, m),
                                  ALU.add).then_inc(s("x1_ready"), 1)

            def tiles(x, m):
                return x[:, m * T:m * T + T, :] if isinstance(m, int) else x[:, bass.ds(m * T, T), :]

            def step(b, p):
                nxt, last = has_next(b), has_last(b)
                if nxt:
                    normalise(b + 1)
                if last:
                    evac_pv(b - 1, 1)
                if nxt:
                    evac_hT(b + 1)
                if last:
                    divide(b - 1, 0)
                if nxt:
                    pieces_keys(b + 1)
                if last:
                    divide(b - 1, 1)
                if nxt:
                    pieces_queries(b + 1)
                evac_pv(b, 0)
                if nxt:
                    evac_stack(b + 1, 1 - p, 0)
                if last:
                    residual1(b - 1)
                if nxt:
                    for k in range(1, 4):
                        evac_stack(b + 1, 1 - p, k)

            for buf in (stackA, stackB):
                dve.memset(buf[:, :, SUMCOL:SLOT], 0.0)
            dve.memset(oh[:, 0, :], 0.0)
            for p in range(2):
                dve.memset(qrysT[p][:, :, :, :], 0.0)
                dve.memset(vaug[p][:, :, :, DH:32], 0.0)
            c = link.mark(dve.memset(rden[:, :, :], 0.0))
            link.wait(c)
            dve.memset(stackA[:, :, SUMCOL + 3:SUMCOL + 9], 1.0)
            dve.memset(stackB[:, :, SUMCOL:SUMCOL + 3], 1.0)
            for p in range(2):
                i = dve.memset(vaug[p][:, :, :, DH:DH + 1], 1.0)
            i.then_inc(s("consts_ready"), 1)
            dve.wait_ge(s("x_first"), 16)
            stats(0, T)
            normalise(0)
            dve.wait_ge(s("attn_weights"), 16 * 10)
            SCALE = float(DH) ** -0.5
            dve.tensor_scalar(s2b[:, :, :], taub[:, :].unsqueeze(2).broadcast_to([P, H, DH]), 2.0 * SCALE, None,
                              ALU.mult)
            for t in range(T):
                dve.tensor_scalar(snegb[:, t, :], taub[:, :], -SCALE, None, ALU.mult)
            link(dve.tensor_tensor(wog_t[:, :], wog_t[:, :], g1b[:, :], ALU.mult))
            evac_hT(0)
            pieces_keys(0)
            pieces_queries(0)
            for k in range(4):
                evac_stack(0, 0, k)
            dve.wait_ge(s("x_rest"), 16)
            stats(T, TILES)
            steps(dve, link, 2 * 11, step)
            m = B - 1
            evac_pv(m, 1)
            divide(m, 0)
            divide(m, 1)
            residual1(m)

            link(dve.tensor_scalar(minus8[:, :], iota8[:, :], float(E), None, ALU.subtract))
            dve.wait_ge(s("chan_weights"), 16 * 6)
            dve.wait_ge(s("x1_ready"), B)
            c = link.mark(dve.tensor_scalar(cols[:, 5:6], cols[:, 4:5], 2.0 / N ** 0.5, None, ALU.mult))
            link(dve.tensor_tensor(wogc[:, :], wogc[:, :], g2b[:, :], ALU.mult))
            for g in range(2):
                a = GT * g
                bn(x1, a, a + GT)
                rsqrt(r1[:, a:a + GT], mv[:, a:a + GT, 1], a, a + GT)
                ge(dve, s("x2T_ready"), GB * g)
                ge(dve, s("tTp_ready"), GB * g)
                for t in range(GT):
                    i = dve.tensor_scalar(tn[:, t, :], x1[:, a + t, :], mv[:, a + t, 0:1], r1[:, a + t:a + t + 1],
                                          ALU.subtract, ALU.mult)
                i.then_inc(s("xn2_ready"), 1)
                for k in range(GB):
                    n = GB * g + k
                    dve.wait_ge(s("x2T_ready"), n + 1)
                    ge(dve, s("x2_ready"), GB * g)
                    dve.tensor_scalar(h2T[:, k, :], banks[2 * k][:, 0:N], cols[:, 2:3], cols[:, 3:4], ALU.mult,
                                      ALU.add).then_inc(s("h2T_ready"), 1)
                for k in range(GB):
                    n = GB * g + k
                    dve.wait_ge(s("sqc_ready"), n + 1)
                    ge(dve, s("gram_ready"), GB * g)
                    dve.tensor_copy(qc[:, k, :], banks[2 * k + 1][:, 0:T * D]).then_inc(s("qc_copied"), 1)
                for k in range(GB):
                    n = GB * g + k
                    dve.wait_ge(s("gram_ready"), n + 1)
                    ge(dve, s("at_ready"), GB * g)
                    link(dve.scalar_tensor_tensor(lg[:, k, :], banks[2 * k][:, 0:D], cols[:, 5:6], mask[:, :],
                                                  ALU.mult, ALU.add))
                    dve.tensor_reduce(nmx[:, k:k + 1], lg[:, k, :], AX_X, ALU.max, negate=True)\
                       .then_inc(s("lg_ready"), 1)
                for k in range(GB):
                    n = GB * g + k
                    dve.wait_ge(s("at_ready"), n + 1)
                    ge(dve, s("wp_ready"), GB * g)
                    link(dve.reciprocal(rsum[:, k:k + 1], ssum[:, k:k + 1]))
                    dve.tensor_scalar(atn[:, k, :], at[:, k, :], rsum[:, k:k + 1], None, ALU.mult)\
                       .then_inc(s("atn_ready"), 1)
                for k in range(GB):
                    n = GB * g + k
                    dve.wait_ge(s("wpp_ready"), n + 1)
                    ge(dve, s("x2_ready"), GB * g)
                    dve.tensor_copy(wpp[:, k, :], banks[2 * k][:, 0:D]).then_inc(s("wpp_copied"), 1)
                dve.wait_ge(s("scaled_ready"), g + 1)
                for k in range(GB):
                    n = GB * g + k
                    dve.wait_ge(s("x2_ready"), n + 1)
                    i = dve.tensor_tensor(rec[:, n * T:n * T + T, D:2 * D],
                                          banks[2 * k + 1][:, 0:N].rearrange("p (t d) -> p t d", t=T),
                                          xin[:, n * T:n * T + T, :], ALU.add)
                    i.then_inc(s("y_ready"), 1)
                dve.wait_ge(s("y_ready"), GB * (g + 1))
                bn(rec[:, :, D:2 * D], a, a + GT)
                rsqrt(r1[:, a:a + GT], mv[:, a:a + GT, 1], a, a + GT)
                for t in range(GT):
                    i = dve.tensor_scalar(rec[:, a + t, 0:D], rec[:, a + t, D:2 * D], mv[:, a + t, 0:1], r1[:, a + t:a + t + 1],
                                          ALU.subtract, ALU.mult)
                i.then_inc(s("tn_ready"), 1)
                dve.wait_ge(s("rl_ready"), g + 1)
                link(dve.tensor_tensor(rl[:, :, :], banks[1][:, 0:GT * E].rearrange("p (t e) -> p t e", e=E),
                                       swb[:, :].unsqueeze(1).broadcast_to([P, GT, E]), ALU.add))
                over_e = lambda x: x[:, :].unsqueeze(2).broadcast_to([P, GT, E])
                over_t = lambda x: x[:, :].unsqueeze(1).broadcast_to([P, GT, E])
                link(dve.tensor_reduce(rmx[:, :], rl[:, :, :], AX_X, ALU.max))
                dve.tensor_tensor(rl[:, :, :], rl[:, :, :], over_e(rmx), ALU.subtract).then_inc(s("rmx_ready"), 1)
                dve.wait_ge(s("re_ready"), g + 1)
                link(dve.tensor_reduce(rmx[:, :], re[:, :, :], AX_X, ALU.max))
                link(dve.tensor_tensor(cand[:, :, :], re[:, :, :], over_e(rmx), ALU.is_equal))
                link(dve.tensor_tensor(cand[:, :, :], cand[:, :, :], over_t(minus8), ALU.mult))
                link(dve.tensor_reduce(first[:, :], cand[:, :, :], AX_X, ALU.min))
                dve.tensor_tensor(oh[:, a + 1:a + GT + 1, :], over_e(first), over_t(minus8), ALU.is_equal)\
                   .then_inc(s("oh_ready"), 1)
                link(dve.reduce_sum(rs[:, :], re[:, :, :], AX_X))
                link(dve.reciprocal(rs[:, :], rs[:, :]))
                link(dve.tensor_tensor(rec[:, a:a + GT, PROB], rs[:, :], rmx[:, :], ALU.mult))
                dve.wait_ge(s("rank_ready"), g + 1)
                link(dve.tensor_tensor(rank[:, :, :], banks[3][:, 0:GT * E].rearrange("p (t e) -> p t e", e=E),
                                       over_t(ebase), ALU.add))
                link(dve.tensor_tensor(rank[:, :, :], rank[:, :, :], oh[:, a + 1:a + GT + 1, :], ALU.mult))
                link(dve.reduce_sum(first[:, :], rank[:, :, :], AX_X))
                dve.tensor_copy(pos[:, a:a + GT], first[:, :]).then_inc(s("pos_ready"), 1)
            count = banks[5][:, 0:E]
            over_j = lambda x: x[:, :].unsqueeze(1).broadcast_to([P, JT, E])
            link(dve.tensor_scalar(cnt_i[:, :], count, float(P - 1), None, ALU.add))
            link(dve.tensor_tensor(ptab[:, :], count, ebase[:, :], ALU.add))
            link(dve.tensor_scalar(cnt_i[:, :], cnt_i[:, :], P.bit_length() - 1, None, ALU.arith_shift_right))
            link(dve.tensor_copy(ntile[:, :], cnt_i[:, :]))
            link(dve.tensor_tensor_scan(cum[:, :], ones8[:, :], ntile[:, :], 0.0, ALU.mult, ALU.add))
            link(dve.tensor_tensor(past[:, :, :], jiota[:, :].unsqueeze(2).broadcast_to([P, JT, E]), over_j(cum),
                                   ALU.is_ge))
            link(dve.reduce_sum(ej[:, :], past[:, :, :], AX_X))
            link(dve.tensor_tensor(past[:, :, :], past[:, :, :], over_j(ntile), ALU.mult))
            link(dve.reduce_sum(rj[:, :], past[:, :, :], AX_X))
            link(dve.tensor_tensor(rj[:, :], jiota[:, :], rj[:, :], ALU.subtract))
            link(dve.tensor_scalar(rj[:, :], rj[:, :], float(P), None, ALU.mult))
            link(dve.scalar_tensor_tensor(rj[:, :], ej[:, :], float(REGION), rj[:, :], ALU.mult, ALU.add))
            link(dve.tensor_scalar(rtab[:, :], rj[:, :], float(E * REGION), None, ALU.min))
            dve.tensor_scalar(etab[:, :], ej[:, :], float(E - 1), None, ALU.min).then_inc(s("table_ready"), 1)

            dve.wait_ge(s("moe_weights"), (2 + E) * 16)
            dve.wait_ge(s("table_ready"), 1)

            def add_b1(j, k):
                ex = dve.value_load(col_at(etab, j), min_val=0, max_val=E - 1)
                dve.wait_ge(s("h_ready"), j + 1)
                ge(dve, s("gelu_ready"), j - 1)
                dve.tensor_tensor(hpre[k % 2][:, :, :], banks[2 + k % 2][:, :].rearrange("p (f t) -> p f t", f=FT),
                                  b1s[:, bass.ds(ex, 1), :].rearrange("p e f -> p (e f)").unsqueeze(2)
                                  .broadcast_to([P, FT, P]), ALU.add).then_inc(s("hpre_ready"), 1)

            def finish(j, k, turn):
                ex = dve.value_load(col_at(etab, j), min_val=0, max_val=E - 1)
                dve.wait_ge(s("z_ready"), j + 1)
                dve.tensor_tensor(zj[k % 2][:, :], banks[4 + k % 2][:, 0:D],
                                  b2b[:, bass.ds(ex, 1), :].rearrange("p e d -> p (e d)"), ALU.add)\
                   .then_inc(s("zj_ready"), 1)
                dve.wait_ge(s("zj_ready"), j + 1)
                dve.wait_ge(s(f"yj_loaded{k}"), turn * 16 + 16)
                dve.scalar_tensor_tensor(at_j(oj, j), zj[k % 2][:, :], at_j(yj, j)[:, PROB - D:PROB - D + 1],
                                         at_j(yj, j)[:, 0:D],
                                         ALU.mult, ALU.add).then_inc(s("o_ready"), 1)

            add_b1(0, 0)

            def step(j, k, turn):
                if ahead(j, 1):
                    add_b1(j + 1, k + 1)
                finish(j, k, turn)

            tiles_of_experts(dve, step)

        @block.tensor
        def _(pe):
            def normT(n):
                pe.wait_ge(s("xn_ready"), n + 1)
                for t in range(T):
                    i = pe.transpose(aux[0][:, t * P:t * P + P], xh[:, t, :], ident[:, :])
                i.then_inc(s("xT_ready"), 1)

            def project_qv(n):
                pe.wait_ge(s("hT_ready"), n + 1)
                ge(pe, s("stT_read"), n * 4 - 1)
                for t in range(T):
                    i = pe.matmul(aux[2][:, t * 2 * D:(t + 1) * 2 * D], hT[:, t * P:t * P + P], wqkv[:, :],
                                  start=True, stop=True)
                i.then_inc(s("qv_ready"), 1)

            def stackT(n, k):
                if k == 0:
                    pe.wait_ge(s("stack_ready"), n + 1)
                    pe.wait_ge(s("sums_ready"), n + 1)
                    pe.wait_ge(s("v_ready"), n + 1)
                    pe.wait_ge(s("q_read"), n + 1)
                if k == 1:
                    ge(pe, s("onT_ready"), n - 1)
                    ge(pe, s("stT_read"), n * 4)
                if k >= 2:
                    pe.wait_ge(s("stT_read"), n * 4 + k - 1)
                bank = auxb[(2, 1, 2, 1)[k]]
                src = stackA if k < 2 else stackB
                for jj in range(4):
                    j = 4 * (k % 2) + jj
                    for t in range(T):
                        h = t * H + 2 * j
                        i = pe.transpose(bank[:, jj * N + t * P:jj * N + t * P + P],
                                         src[:, h:h + 2, :].rearrange("p h c -> p (h c)"), identb[:, :])
                i.then_inc(s("stT_ready"), 1)

            def logits(b, p, j):
                if j == 0:
                    pe.wait_ge(s("stT_read"), b * 4 + 4)
                ge(pe, s("exp_ready"), b * 8 + j - 1)
                for t in range(T):
                    i = pe.matmul(logit_banks[j % 2][t][:, :], keysT[p][:, j, t * P:t * P + P],
                                  qrysT[p][:, j, :, :].rearrange("p e n -> p (e n)"), start=True, stop=True)
                i.then_inc(s("logits_ready"), 1)

            def pv(b, p, g):
                pe.wait_ge(s("exp_ready"), b * 8 + 2 * g + 2)
                if g % 2 == 0:
                    ge(pe, s("o_read"), b * 2 + g // 2)
                for t in range(T):
                    for jj in range(4):
                        i = pe.matmul(pv_bank[32 * jj:32 * jj + 32, (g % 2) * N:(g % 2) * N + N],
                                      vaug[p][:, t, 4 * g + jj, :], expo[(2 * g + jj // 2) % 4][:, t, jj % 2, :],
                                      start=(t == 0), stop=(t == T - 1))
                i.then_inc(s("pv_done"), 1)

            def oT_back(m, half):
                pe.wait_ge(s("o_read"), m * 2 + half + 1)
                if half == 0:
                    pe.wait_ge(s("stT_read"), min(m + 2, B) * 4 if isinstance(m, int) else m * 4 + 8)
                for t in range(T):
                    for gg in range(2):
                        i = pe.transpose(aux[1 - half][:, (t * 2 + gg) * P:(t * 2 + gg) * P + P],
                                         oT[:, 2 * half + gg, t * P:t * P + P], ident[:, :])
                i.then_inc(s("oT_ready"), 1)

            def onT_(m):
                pe.wait_ge(s("on_ready"), m * 2 + 2)
                for t in range(T):
                    i = pe.transpose(aux[1][:, t * P:t * P + P], on[:, t, :, :].rearrange("p h d -> p (h d)"),
                                     ident[:, :])
                i.then_inc(s("onTp_ready"), 1)

            def project_o(m):
                pe.wait_ge(s("onT_ready"), m + 1)
                for t in range(T):
                    i = pe.matmul(aux[0][:, t * D:t * D + D], onT[:, t * P:t * P + P], wog_t[:, :], start=True,
                                  stop=True)
                i.then_inc(s("proj_ready"), 1)

            def step(b, p):
                nxt, last = has_next(b), has_last(b)
                m, n = b - 1, b + 1
                logits(b, p, 0)
                if nxt:
                    normT(n)
                if last:
                    pv(m, 1 - p, 3)
                logits(b, p, 1)
                if last:
                    oT_back(m, 0)
                if nxt:
                    project_qv(n)
                logits(b, p, 2)
                if last:
                    oT_back(m, 1)
                pv(b, p, 0)
                logits(b, p, 3)
                if last:
                    onT_(m)
                logits(b, p, 4)
                pv(b, p, 1)
                if last:
                    project_o(m)
                logits(b, p, 5)
                if nxt:
                    stackT(n, 0)
                    stackT(n, 1)
                logits(b, p, 6)
                pv(b, p, 2)
                if nxt:
                    stackT(n, 2)
                logits(b, p, 7)
                if nxt:
                    stackT(n, 3)

            pe.wait_ge(s("ident_ready"), 2)
            pe.wait_ge(s("attn_weights"), 16 * 10)
            normT(0)
            project_qv(0)
            for k in range(4):
                stackT(0, k)
            steps(pe, None, 0, step)
            m = B - 1
            pv(m, 1, 3)
            oT_back(m, 0)
            oT_back(m, 1)
            onT_(m)
            project_o(m)

            pe.wait_ge(s("chan_weights"), 16 * 6)
            pe.wait_ge(s("consts_ready"), 9)
            pe.wait_ge(s("x1_ready"), B)
            for g in range(2):
                pe.wait_ge(s("xn2_ready"), g + 1)
                for k in range(GB):
                    for t in range(T):
                        i = pe.transpose(banks[2 * k][:, t * P:t * P + P], tn[:, k * T + t, :], ident[:, :])
                    i.then_inc(s("x2T_ready"), 1)
                for k in range(GB):
                    pe.wait_ge(s("h2T_ready"), GB * g + k + 1)
                    for t in range(T):
                        i = pe.matmul(banks[2 * k + 1][:, t * D:t * D + D], h2T[:, k, t * P:t * P + P], wqkc[:, :],
                                      start=True, stop=True)
                    i.then_inc(s("qc_ready"), 1)
                for k in range(GB):
                    pe.wait_ge(s("qc_copied"), GB * g + k + 1)
                    o = banks[2 * k][:, 0:D]
                    for t in range(T):
                        q_, q2_ = qc[:, k, t * D:t * D + D], sqc[:, k, t * D:t * D + D]
                        pe.matmul(o, q_, q_, start=(t == 0), stop=False)
                        pe.matmul(o, nhalf[:, :], q2_, start=False, stop=False)
                        i = pe.matmul(o, q2_, nhalf[:, :], start=False, stop=(t == T - 1))
                    i.then_inc(s("gram_ready"), 1)
                for k in range(GB):
                    pe.wait_ge(s("atn_ready"), GB * g + k + 1)
                    pe.matmul(banks[2 * k + 1][:, 0:D], atn[:, k, :], wogc[:, :], start=True, stop=True)\
                      .then_inc(s("wp_ready"), 1)
                for k in range(GB):
                    pe.wait_ge(s("wp_copied"), GB * g + k + 1)
                    pe.matmul(banks[2 * k][:, 0:D], wvTc[:, :], wp[:, k, :], start=True, stop=True)\
                      .then_inc(s("wpp_ready"), 1)
                for k in range(GB):
                    pe.wait_ge(s("wpp_copied"), GB * g + k + 1)
                    for t in range(T):
                        i = pe.matmul(banks[2 * k + 1][:, t * D:t * D + D], h2T[:, k, t * P:t * P + P], wpp[:, k, :],
                                      start=True, stop=True)
                    i.then_inc(s("x2_ready"), 1)
                pe.wait_ge(s("tn_ready"), g + 1)
                for k in range(GB):
                    for t in range(T):
                        i = pe.transpose(banks[2 * k][:, t * P:t * P + P], rec[:, GT * g + k * T + t, 0:D], ident[:, :])
                    i.then_inc(s("tTp_ready"), 1)
                for k in range(GB):
                    pe.wait_ge(s("tT_ready"), GB * g + k + 1)
                    for t in range(T):
                        i = pe.matmul(banks[1][:, (k * T + t) * E:(k * T + t) * E + E], tT[:, k, t * P:t * P + P],
                                      sww[:, :], start=True, stop=True)
                i.then_inc(s("rl_ready"), 1)
                pe.wait_ge(s("oh_ready"), g + 1)
                a = GT * g
                oh2 = lambda u, v: oh[:, u + 1:v + 1, :].rearrange("p t e -> p (t e)")
                for back in range(1, a + GT):
                    u = max(back, a) if back > 1 else a
                    pe.matmul(banks[3][:, (u - a) * E:GT * E], onesb[:, :], oh2(u - back, a + GT - back),
                              start=(back == 1), stop=False, skip_group_check=True)
                i = pe.matmul(banks[3][:, 0:GT * E], before[:, :], oh2(a, a + GT), start=False, stop=True,
                              skip_group_check=True)
                if g == 1:
                    for k in range(TILES):
                        i = pe.matmul(banks[5][:, 0:E], onesb[:, :], oh2(k, k + 1), start=(k == 0),
                                      stop=(k == TILES - 1))
                i.then_inc(s("rank_ready"), 1)

            def tokensT(j, k, turn):
                pe.wait_ge(s(f"tj_loaded{k}"), turn * 16 + 16)
                pe.transpose(banks[k % 2][:, 0:P], tj[k][:, :], ident[:, :]).then_inc(s("tj_ready"), 1)

            def layer1(j, k, turn):
                pe.wait_ge(s(f"w1_loaded{k}"), turn * 16 + 16)
                pe.wait_ge(s("tTj_ready"), j + 1)
                ge(pe, s("hpre_ready"), j - 1)
                for f in range(FT):
                    i = pe.matmul(banks[2 + k % 2][:, f * P:f * P + P], w1j[k][:, f * P:f * P + P], tTj[k % 2][:, :],
                                  start=True, stop=True)
                i.then_inc(s("h_ready"), 1)

            def layer2(j, k):
                ex = pe.value_load(col_at(etab, j), min_val=0, max_val=E - 1)
                pe.wait_ge(s("gelu_ready"), j + 1)
                ge(pe, s("o_ready"), j - 1)
                for f in range(FT):
                    i = pe.matmul(banks[4 + k % 2][:, 0:D], hj[k % 2][:, f, :],
                                  w2s[:, bass.ds(ex, 1), f, :].rearrange("p e d -> p (e d)"), start=(f == 0),
                                  stop=(f == FT - 1))
                i.then_inc(s("z_ready"), 1)

            pe.wait_ge(s("table_ready"), 1)
            pe.wait_ge(s("moe_weights"), (2 + E) * 16)
            tokensT(0, 0, 0)
            tokensT(1, 1, 0)
            layer1(0, 0, 0)

            def step(j, k, turn):
                if ahead(j, 2):
                    tokensT(j + 2, (k + 2) % RING, turn + (k + 2) // RING)
                if ahead(j, 1):
                    layer1(j + 1, (k + 1) % RING, turn + (k + 1) // RING)
                layer2(j, k)

            tiles_of_experts(pe, step)


def kernel(**inputs):
    import numpy as _np
    import concourse.bacc as _bacc
    from concourse import mybir as _mybir
    from concourse.bass_utils import run_bass_kernel_spmd as _run

    a = {k.split("_", 2)[2]: _np.asarray(v) for k, v in inputs.items()}
    col = lambda v: v.reshape(-1, 1)
    laid = [
        ("x", a["x"]), ("wqk_t", a["Wqk_t"]), ("wv_t", a["Wv_t"]), ("wo_t", a["Wo_t"]), ("tau_t", a["tau_t"].reshape(-1)),
        ("wqk_c", a["Wqk_c"]), ("wvT_c", a["Wv_c"].T), ("wo_c", a["Wo_c"]),
        ("tau_c", col(_np.repeat(a["tau_c"].reshape(-1), CDH))),
        ("ln1_w", col(a["ln1_w"])), ("ln1_b", col(a["ln1_b"])), ("ln2_w", col(a["ln2_w"])), ("ln2_b", col(a["ln2_b"])),
        ("gamma1", a["gamma1"]), ("gamma2", a["gamma2"]), ("switch_w", a["switch_w"]), ("switch_b", a["switch_b"]),
        ("w1", a["w1"]), ("b1T", a["b1"].reshape(E * FT, P).T), ("w2", a["w2"]), ("b2", a["b2"]),
    ]
    nc = _bacc.Bacc("TRN2", target_bir_lowering=False, num_devices=1)
    arrays, args = {}, []
    for name, v in laid:
        v = _np.ascontiguousarray(v)
        arrays[f"in_{name}"] = v
        args.append(nc.dram_tensor(f"in_{name}", v.shape, _mybir.dt.from_np(v.dtype), kind="ExternalInput").ap())
    args.append(nc.dram_tensor("out_0", (B, N, D), F32, kind="ExternalOutput").ap())
    build(nc, *args)
    r = _run(nc, [arrays], core_ids=[0])
    return r.results[0]["out_0"]
```

```python
from contextlib import ExitStack

import concourse.bass as bass
from concourse import mybir

P = 128
F32 = mybir.dt.float32
BF16 = mybir.dt.bfloat16
I32 = mybir.dt.int32
ALU = mybir.AluOpType
ACT = mybir.ActivationFunctionType
AX_X = mybir.AxisListType.X

EPS = 1e-5
B, N, D = 8, 256, 128
H, DH = 16, 8
CH, CDH = 8, 16
E, F = 8, 512
T = N // P
TILES = B * T
PAIRS = H // 2
GROUPS = H // 4
SLOT = 64
SUMCOL = 6 * DH
NEG = -1.0e30
FT = F // P
REGION = B * N + P
NSLOT = E * REGION + P
REC = 2 * D + 2
PROB, IDENT = 2 * D, 2 * D + 1
JT = (B * N + E * (P - 1)) // P
RING, LOOKAHEAD = 4, 3
NOBODY = 4095
MAGIC = float(0x5F3759DF)


class Link:

    def __init__(self, eng, sem):
        self.eng, self.sem, self.n, self.turn, self.per = eng, sem, 0, None, 0

    def loop(self, i, per):
        self.turn, self.per, self.at = i, per, self.n

    def end(self, turns):
        assert self.n - self.at == self.per, self.n - self.at
        self.n, self.turn = self.at + self.per * turns, None

    def value(self):
        return self.n if self.turn is None else self.turn * self.per + self.n

    def mark(self, ins):
        ins.then_inc(self.sem, 1)
        self.n += 1
        return self.value()

    def wait(self, value):
        self.eng.wait_ge(self.sem, value)

    def __call__(self, ins):
        self.wait(self.mark(ins))


def ge(eng, sem, value):
    if not isinstance(value, int) or value > 0:
        eng.wait_ge(sem, value)


def build(nc, x_in, wqk_t, wv_t, wo_t, tau_t, wqk_c, wvT_c, wo_c, tau_c, ln1_w, ln1_b, ln2_w, ln2_b,
          gamma1, gamma2, switch_w, switch_b, w1, b1T, w2, b2, out):
    with ExitStack() as ctx:
        def sb(name, shape, dt=F32):
            return ctx.enter_context(nc.sbuf_tensor(name, shape, dt))

        def sem(name):
            return ctx.enter_context(nc.semaphore(name))

        psum = ctx.enter_context(nc.psum_tensor("psum", [P, 8, 512], F32))
        banks = [psum[:, i, :] for i in range(8)]
        logit_banks = [banks[0:2], banks[2:4]]
        pv_bank = banks[4]
        aux = banks[5:8]
        auxb = [a.bitcast(BF16) for a in aux]

        xin = sb("xin", [P, TILES, D])
        x0 = sb("x0", [P, TILES, D])
        x1 = sb("x1", [P, TILES, D])
        ident = sb("ident", [P, P])
        identb = sb("identb", [P, P], BF16)
        bn6 = sb("bn6", [P, TILES, 6])
        mv = sb("mv", [P, TILES, 2])
        ve = sb("ve", [P, 2, TILES])
        ri = sb("ri", [P, 2, TILES], I32)
        rt = sb("rt", [P, 2, TILES])
        hv = sb("hv", [P, 2, TILES])
        half_c = sb("half_c", [P, 2])
        rr = sb("rr", [P, 2, TILES])
        wqkv = sb("wqkv", [P, 2 * D])
        wog_t = sb("wog_t", [P, D])
        g1b = sb("g1b", [P, D])
        cols = sb("cols", [P, 8])
        taub = sb("taub", [P, H])
        s2b = sb("s2b", [P, H, DH])
        snegb = sb("snegb", [P, T, H])
        xh = sb("xh", [P, T, D])
        hT = sb("hT", [P, N])
        qs = sb("qs", [P, T, D])
        vs = sb("vs", [P, T, D])
        sq = sb("sq", [P, T, D])
        ra = sb("ra", [P, T * H, DH])
        pf = sb("pf", [P, T * H, DH])
        rb = sb("rb", [P, T * H, DH])
        c0 = sb("c0", [P, T * H])
        cf = sb("cf", [P, T * H])
        rc = sb("rc", [P, T * H])
        ones = sb("ones", [P, T * H])
        stackA = sb("stackA", [P, T * H, SLOT], BF16)
        stackB = sb("stackB", [P, T * H, SLOT], BF16)
        arena = sb("arena", [P, 8 * T * N + 3 * PAIRS * N])
        expo_all = arena[:, 0:8 * T * N]
        keys_all = arena[:, 8 * T * N:8 * T * N + PAIRS * N]
        qrys_all = arena[:, 8 * T * N + PAIRS * N:8 * T * N + 3 * PAIRS * N]
        keysT = [keys_all.bitcast(BF16).rearrange("p (q j n) -> p q j n", q=2, n=N)[:, q] for q in range(2)]
        qrysT = [qrys_all.bitcast(BF16).rearrange("p (q j e n) -> p q j e n", q=2, e=2, n=N)[:, q]
                 for q in range(2)]
        vaug = [sb(f"vaug{p}", [P, T, H, 32]) for p in range(2)]
        expo = [expo_all[:, i * T * 2 * N:(i + 1) * T * 2 * N].rearrange("p (t e n) -> p t e n", t=T, e=2)
                for i in range(4)]
        oT = sb("oT", [P, GROUPS, N])
        rden = sb("rden", [P, T, H])
        on = sb("on", [P, T, H, DH])
        onT = sb("onT", [P, N])
        wqkc = sb("wqkc", [P, D])
        wvTc = sb("wvTc", [P, D])
        wogc = sb("wogc", [P, D])
        g2b = sb("g2b", [P, D])
        mask = sb("mask", [P, D])
        nhalf = sb("nhalf", [P, D])
        UNITS, UB = B // 2, 2
        UT = UB * T
        GT = TILES // 2
        h2T = qrys_all[:, 0:B * N].rearrange("p (u x) -> p u x", u=UNITS)
        tT = qrys_all[:, B * N:2 * B * N].rearrange("p (u x) -> p u x", u=UNITS)
        sqc = keys_all[:, 0:B * N].rearrange("p (u x) -> p u x", u=UNITS)
        tn = sb("tn", [P, TILES, D])
        qc = expo_all[:, B * N:2 * B * N].rearrange("p (u x) -> p u x", u=UNITS)
        lg = sb("lg", [P, B, D])
        nmx = sb("nmx", [P, B])
        ssum = sb("ssum", [P, B])
        rsum = sb("rsum", [P, B])
        at = sb("at", [P, B, D])
        atn = sb("atn", [P, B, D])
        wp = sb("wp", [P, B, D])
        wpp = sb("wpp", [P, B, D])
        mvB = sb("mvB", [P, TILES, 2])
        shift = sb("shift", [P, 2, TILES])
        rec = sb("rec", [P, TILES, REC])
        warm = sb("warm", [P, 1])
        sww = sb("sww", [P, E])
        swb = sb("swb", [P, E])
        rl = sb("rl", [P, TILES, E])
        rmx = sb("rmx", [P, TILES])
        re = sb("re", [P, TILES, E])
        rs = sb("rs", [P, GT])
        iota8 = sb("iota8", [P, E])
        ebase = sb("ebase", [P, E])
        minus8 = sb("minus8", [P, E])
        jiota = sb("jiota", [P, JT])
        cand = sb("cand", [P, GT, E])
        first = sb("first", [P, GT])
        oh = sb("oh", [P, 1 + TILES, E], BF16)
        before = sb("before", [P, P], BF16)
        onesb = sb("onesb", [P, P], BF16)
        rank = sb("rank", [P, GT, E])
        pos = sb("pos", [P, TILES], I32)
        ones8 = sb("ones8", [P, E])
        cnt_i = sb("cnt_i", [P, E], I32)
        ntile = sb("ntile", [P, E])
        cum = sb("cum", [P, E])
        past = sb("past", [P, JT, E])
        ej = sb("ej", [P, JT])
        b1j = sb("b1j", [P, JT, FT])
        rj = sb("rj", [P, JT])
        etab = sb("etab", [P, JT], I32)
        rtab = sb("rtab", [P, JT], I32)
        ptab = sb("ptab", [P, E], I32)
        padrec = sb("padrec", [P, REC])
        b1s = sb("b1s", [P, E, FT])
        b2b = sb("b2b", [P, E, D])
        w2s = sb("w2s", [P, E, FT, D])
        w1s = sb("w1s", [P, E, F])
        w1j = [sb(f"w1j{i}", [P, F]) for i in range(RING)]
        tj = [sb(f"tj{i}", [P, D]) for i in range(2)]
        tTj = [sb(f"tTj{i}", [P, P]) for i in range(2)]
        hpre = [sb(f"hpre{i}", [P, FT, P]) for i in range(2)]
        hj = [sb(f"hj{i}", [P, FT, P]) for i in range(2)]
        zj = [sb(f"zj{i}", [P, D]) for i in range(2)]
        recj = arena[:, 0:JT * REC].rearrange("p (j c) -> p j c", c=REC)
        b1e = arena[:, JT * (REC + D):JT * (REC + D + FT * E)].rearrange("p (j f e) -> p j f e", f=FT, e=E)
        oj = arena[:, JT * REC:JT * (REC + D)].rearrange("p (j d) -> p j d", d=D)
        slots = nc.dram_tensor("slots", (NSLOT, REC), F32).ap()

        S = {}

        def s(name):
            if name not in S:
                S[name] = sem(name)
            return S[name]

        for names in (
                "x_first x_rest attn_weights chan_weights moe_weights ident_ready consts_ready zeros_ready",
                "pool_link dve_link zj_ready",
                "rest_seeded rest_scaled tn_seeded tn_scaled scale2_ready scale3_ready",
                "xn_ready xT_ready hT_ready qv_ready q_ready vs_ready v_ready sq_ready sum_ready sums_ready "
                "keys_ready qrys_ready stT_ready stack_read keys1_read logits_ready exp_ready pv_done o_read "
                "oT_ready on_ready onTp_ready onT_ready proj_ready x1_ready scaled_ready",
                "xn2_dve xn2_act x2T_ready h2T_ready qc_ready qc_copied sqc_ready gram_ready lg_ready at_ready "
                "atn_ready wp_ready wp_copied wpp_ready wpp_copied x2_ready y_ready",
                "tn_dve tn_act tTp_ready tT_ready rl_ready rmx_ready re_ready oh_ready rank_ready pos_ready "
                "ids_ready pad_ready pads_placed table_ready sorted padded",
                "rec_loaded0 rec_loaded1 rec_loaded2 rec_loaded3 tj_copied tj_ready tTj_ready w1_copied h_ready "
                "hpre_ready gelu_ready z_ready o_ready out_written"):
            for name in names.split():
                s(name)

        block = ctx.enter_context(nc.Block())

        def steps(eng, link, per, step):
            turns = (B - 4) // 2
            step(0, 0)
            with eng.Fori(0, turns) as i:
                if link:
                    link.loop(i, per)
                step(i * 2 + 1, 1)
                step(i * 2 + 2, 0)
            if link:
                link.end(turns)
            for b in range(2 * turns + 1, B):
                step(b, b % 2)

        def col_at(table, j):
            return table[0:1, j:j + 1] if isinstance(j, int) else table[0:1, bass.ds(j, 1)]

        def at_j(x, j):
            return x[:, j, :] if isinstance(j, int) else x[:, bass.ds(j, 1), :].rearrange("p a d -> p (a d)")

        def tiles_of_experts(eng, step):
            for k in range(RING):
                step(k, k, 0)
            turns = (JT - LOOKAHEAD) // RING
            with eng.Fori(1, turns) as j4:
                for k in range(RING):
                    step(j4 * RING + k, k, j4)
            for j in range(turns * RING, JT):
                step(j, j % RING, j // RING)

        def ahead(j, n):
            return not isinstance(j, int) or j + n < JT

        def qv_bank(n):
            return banks[0] if isinstance(n, int) and n == 1 else aux[2]

        has_second = lambda b: not isinstance(b, int) or b + 2 < B
        has_next = lambda b: not isinstance(b, int) or b + 1 < B
        has_last = lambda b: not isinstance(b, int) or b > 0

        def pad_rows(eng, a, b_):
            eng.wait_ge(s("pads_placed"), 1)
            for e in range(a, b_):
                row = eng.value_load(ptab[0:1, e:e + 1], min_val=e * REGION, max_val=e * REGION + B * N)
                eng.dma_start(slots[bass.ds(row, P), :], padrec[:, :]).then_inc(s("padded"), 16)

        @block.sync
        def _(sp):
            xv = x_in.rearrange("b (t p) d -> p (b t) d", p=P)
            sp.dma_start(xin[:, 0:2 * T, :], xv[:, 0:2 * T, :]).then_inc(s("x_first"), 16)
            sp.dma_start(wqkv[:, 0:D], wqk_t).then_inc(s("attn_weights"), 16)
            sp.dma_start(wqkv[:, D:2 * D], wv_t).then_inc(s("attn_weights"), 16)
            for k, v in enumerate((ln1_w, ln1_b, ln2_w, ln2_b, tau_c)):
                sp.dma_start(cols[:, k:k + 1], v).then_inc(s("attn_weights"), 16)
            sp.dma_start(taub[:, :], tau_t.partition_broadcast(P)).then_inc(s("attn_weights"), 16)
            sp.dma_start(g1b[:, :], gamma1.partition_broadcast(P)).then_inc(s("attn_weights"), 16)
            sp.dma_start(wog_t[:, :], wo_t).then_inc(s("attn_weights"), 16)
            sp.dma_start(xin[:, 2 * T:, :], xv[:, 2 * T:, :]).then_inc(s("x_rest"), 16)
            sp.dma_start(wqkc[:, :], wqk_c).then_inc(s("chan_weights"), 16)
            sp.dma_start(wvTc[:, :], wvT_c).then_inc(s("chan_weights"), 16)
            sp.dma_start(wogc[:, :], wo_c).then_inc(s("chan_weights"), 16)
            sp.dma_start(g2b[:, :], gamma2.partition_broadcast(P)).then_inc(s("chan_weights"), 16)
            sp.dma_start(sww[:, :], switch_w).then_inc(s("chan_weights"), 16)
            sp.dma_start(swb[:, :], switch_b.partition_broadcast(P)).then_inc(s("chan_weights"), 16)
            sp.dma_start(b1s[:, :], b1T).then_inc(s("moe_weights"), 16)
            sp.dma_start(b2b[:, :, :].rearrange("p e d -> p (e d)"),
                         b2.rearrange("e d -> (e d)").partition_broadcast(P)).then_inc(s("moe_weights"), 16)
            sp.dma_start(w2s[:, :, :, :].rearrange("p e t d -> p (e t) d"),
                         w2.rearrange("e (t p) d -> p (e t) d", p=P)).then_inc(s("moe_weights"), 16)
            sp.dma_start(w1s[:, :, :], w1.rearrange("e d f -> d e f")).then_inc(s("moe_weights"), 16)
            sp.wait_ge(s("pad_ready"), 2)
            sp.dma_start(slots[E * REGION:NSLOT, :], padrec[:, :]).then_inc(s("padded"), 16)
            pad_rows(sp, 0, E // 2)

            def load_rec(j, k, turn):
                row = sp.value_load(col_at(rtab, j), min_val=0, max_val=NSLOT - P)
                ge(sp, s("tj_copied"), j - RING + 1)
                sp.dma_start(at_j(recj, j), slots[bass.ds(row, P), :]).then_inc(s(f"rec_loaded{k}"), 16)

            sp.wait_ge(s("table_ready"), 1)
            sp.wait_ge(s("sorted"), TILES * 16)
            sp.wait_ge(s("padded"), (E + 1) * 16)
            tiles_of_experts(sp, lambda j, k, turn: load_rec(j, k, turn))
            sp.wait_ge(s("out_written"), JT * 16)

        @block.gpsimd
        def _(pool):
            link = Link(pool, s("pool_link"))
            pool.memset(ident[:, :], 0.0).then_inc(s("pool_link"), 1)
            pool.memset(identb[:, :], 0.0).then_inc(s("pool_link"), 1)
            link.n = 2
            link.wait(2)
            for m in (ident, identb):
                pool.affine_select(out=m[:, :], in_=m[:, :], compare_op=ALU.not_equal, fill=1.0, base=0,
                                   pattern=[[-1, P]], channel_multiplier=1).then_inc(s("ident_ready"), 1)
            link(pool.memset(ones[:, :], 1.0))
            pool.memset(nhalf[:, :], -0.5).then_inc(s("consts_ready"), 1)
            for p in range(2):
                link(pool.memset(vaug[p][:, :, :, DH:32], 0.0))
                pool.memset(vaug[p][:, :, :, DH:DH + 1], 1.0).then_inc(s("zeros_ready"), 1)
                pool.memset(qrysT[p][:, :, :, :], 0.0).then_inc(s("zeros_ready"), 1)
            link(pool.memset(half_c[:, 0:1], 0.5))
            link(pool.memset(half_c[:, 1:2], 1.5))
            link(pool.memset(mask[:, :], 0.0))
            mv3 = mask[:, :].rearrange("p (k c) -> p k c", c=CDH)
            link(pool.affine_select(out=mv3, in_=mv3, compare_op=ALU.is_ge, fill=NEG, base=0,
                                    pattern=[[-CDH, CH], [0, CDH]], channel_multiplier=1))
            pool.affine_select(out=mv3, in_=mv3, compare_op=ALU.is_ge, fill=NEG, base=CDH - 1,
                               pattern=[[CDH, CH], [0, CDH]], channel_multiplier=-1).then_inc(s("consts_ready"), 1)
            for row, step_, size in ((iota8, 1, E), (ebase, REGION, E), (jiota, 1, JT)):
                pool.iota(row[:, :], pattern=[[step_, size]], base=0, channel_multiplier=0,
                          allow_small_or_imprecise_dtypes=True).then_inc(s("consts_ready"), 1)
            pool.iota(rec[:, :, IDENT].bitcast(I32), pattern=[[P, TILES]], base=0, channel_multiplier=1)\
                .then_inc(s("ids_ready"), 1)
            link(pool.memset(before[:, :], 1.0))
            pool.affine_select(out=before[:, :], in_=before[:, :], compare_op=ALU.is_ge, fill=0.0, base=-1,
                               pattern=[[1, P]], channel_multiplier=-1).then_inc(s("consts_ready"), 1)
            pool.memset(onesb[:, :], 1.0).then_inc(s("consts_ready"), 1)
            pool.memset(ones8[:, :], 1.0).then_inc(s("consts_ready"), 1)
            pool.memset(padrec[:, 0:IDENT], 0.0).then_inc(s("pad_ready"), 1)
            pool.memset(padrec[:, IDENT:REC].bitcast(I32), NOBODY).then_inc(s("pad_ready"), 1)

            def copy(dst, src):
                return pool.tensor_tensor(dst, src, ones[:, :].unsqueeze(2).broadcast_to([P, T * H, src.shape[2]]), ALU.mult)

            def sum_pieces(n):
                pool.wait_ge(s("sum_ready"), n + 1)
                ge(pool, s("stT_ready"), n * 4)
                link(copy(stackA[:, :, SUMCOL:SUMCOL + 1], cf[:, :].unsqueeze(2)))
                link(pool.tensor_tensor(rc[:, :].unsqueeze(2), cf[:, :].unsqueeze(2),
                                        stackA[:, :, SUMCOL:SUMCOL + 1], ALU.subtract))
                link(copy(stackA[:, :, SUMCOL + 1:SUMCOL + 2], rc[:, :].unsqueeze(2)))
                ins = pool.tensor_tensor(stackA[:, :, SUMCOL + 2:SUMCOL + 3], rc[:, :].unsqueeze(2),
                                         stackA[:, :, SUMCOL + 1:SUMCOL + 2], ALU.subtract)
                ins.then_inc(s("sums_ready"), 1)
                pool.wait_ge(s("sums_ready"), n * 2 + 1)
                copy(stackB[:, :, SUMCOL + 3:SUMCOL + 6], stackA[:, :, SUMCOL:SUMCOL + 3])\
                    .then_inc(s("sums_ready"), 1)

            def values(n, q):
                pool.wait_ge(s("vs_ready"), n + 1)
                ge(pool, s("pv_done"), n * 4 - 4)
                copy(vaug[q][:, :, :, 0:DH].rearrange("p t h d -> p (t h) d"),
                     vs[:, :, :].rearrange("p t (h d) -> p (t h) d", d=DH)).then_inc(s("v_ready"), 1)

            def squares(n):
                pool.wait_ge(s("q_ready"), n + 1)
                ge(pool, s("sum_ready"), n)
                pool.tensor_tensor(sq[:, :, :], qs[:, :, :], qs[:, :, :], ALU.mult).then_inc(s("sq_ready"), 1)

            mul = lambda dst, x, y: link(pool.tensor_tensor(dst, x, y, ALU.mult))

            def newton(w, k, done=None):
                const = lambda c: half_c[:, c:c + 1].unsqueeze(2).broadcast_to([P, w.stop - w.start, k.stop - k.start])
                mul(hv[:, w, k], ve[:, w, k], const(0))
                g = ri[:, w, k].bitcast(F32)
                for step in range(3):
                    mul(rt[:, w, k], g, g)
                    mul(rt[:, w, k], rt[:, w, k], hv[:, w, k])
                    link(pool.tensor_tensor(rt[:, w, k], const(1), rt[:, w, k], ALU.subtract))
                    i = pool.tensor_tensor(rr[:, w, k], g, rt[:, w, k], ALU.mult)
                    if done and step == 2:
                        i.then_inc(s(done), 1)
                    else:
                        link(i)
                    g = rr[:, w, k]

            squares(0)
            sum_pieces(0)
            values(0, 0)
            squares(1)
            pool.wait_ge(s("rest_seeded"), 1)
            k = slice(2 * T, TILES)
            newton(slice(0, 2), k)
            mul(rt[:, 0, k], rr[:, 0, k], ve[:, 0, k])
            pool.tensor_tensor(rr[:, 1, k], rr[:, 1, k], rt[:, 0, k], ALU.mult).then_inc(s("rest_scaled"), 1)
            sum_pieces(1)

            def step(b, p):
                if has_next(b):
                    values(b + 1, 1 - p)
                if has_second(b):
                    squares(b + 2)
                    sum_pieces(b + 2)

            steps(pool, link, 6, step)
            def square_qc(u):
                pool.wait_ge(s("qc_copied"), u + 1)
                pool.tensor_tensor(sqc[:, u, :], qc[:, u, :], qc[:, u, :], ALU.mult).then_inc(s("sqc_ready"), 1)

            for g in range(2):
                pool.wait_ge(s("x1_ready"), GT // T * (g + 1))
                pool.tensor_tensor(xin[:, GT * g:GT * g + GT, :], x1[:, GT * g:GT * g + GT, :],
                                   xin[:, GT * g:GT * g + GT, :], ALU.add).then_inc(s("scaled_ready"), 1)
                square_qc(2 * g)
                square_qc(2 * g + 1)
            pool.wait_ge(s("tn_seeded"), 1)
            newton(slice(1, 2), slice(0, GT), "tn_scaled")
            pool.wait_ge(s("ids_ready"), 1)
            for g in range(2):
                pool.wait_ge(s("pos_ready"), g + 1)
                for k in range(GT * g, GT * g + GT):
                    pool.indirect_dma_start(slots[:, :], bass.IndirectOffsetOnAxis(ap=pos[:, k:k + 1], axis=0),
                                            rec[:, k, :], None).then_inc(s("sorted"), 16)

            out_rows = out.rearrange("b n d -> (b n) d")

            last_row = pool.to_reg(B * N - 1)

            def send(j, k):
                pool.wait_ge(s("o_ready"), j + 1)
                pool.indirect_dma_start(out_rows, bass.IndirectOffsetOnAxis(ap=recj[:, j, IDENT:].bitcast(I32), axis=0),
                                        oj[:, j, :], None, bounds_check=last_row, oob_is_err=False)\
                    .then_inc(s("out_written"), 16)

            for j in range(JT):
                send(j, j % RING)

        @block.scalar
        def _(act):
            def evac_qv(n):
                act.wait_ge(s("qv_ready"), n + 1)
                ge(act, s("keys_ready"), n)
                ge(act, s("sq_ready"), n)
                qv = qv_bank(n)[:, :].rearrange("p (t w d) -> p w t d", t=T, w=2)
                act.activation(qs[:, :, :], qv[:, 0], ACT.Copy).then_inc(s("q_ready"), 1)
                ge(act, s("v_ready"), n)
                act.activation(vs[:, :, :], qv[:, 1], ACT.Copy).then_inc(s("vs_ready"), 1)

            def exps(b, j):
                act.wait_ge(s("logits_ready"), b * 8 + j + 1)
                ge(act, s("pv_done"), b * 4 + (j - 4) // 2 + 1)
                act.activation(expo[j % 4][:, :, :, :].rearrange("p t e n -> p t (e n)"),
                               lg_view(j % 2), ACT.Exp).then_inc(s("exp_ready"), 1)

            def lg_view(k):
                return psum[:, 2 * k:2 * k + 2, :]

            def evac_hT(n):
                act.wait_ge(s("xT_ready"), n + 1)
                ge(act, s("qv_ready"), n)
                act.activation(hT[:, :], aux[0][:, 0:N], ACT.Identity, bias=cols[:, 1:2], scale=cols[:, 0:1])\
                   .then_inc(s("hT_ready"), 1)

            def evac_pv(b, half):
                act.wait_ge(s("pv_done"), b * 4 + 2 * half + 2)
                if half == 0:
                    ge(act, s("oT_ready"), b * 2)
                act.activation(oT[:, 2 * half:2 * half + 2, :].rearrange("p g n -> p (g n)"), pv_bank[:, :], ACT.Copy)\
                   .then_inc(s("o_read"), 1)

            def evac_onT(m):
                act.wait_ge(s("onTp_ready"), m + 1)
                act.activation(onT[:, :], aux[1][:, 0:N], ACT.Copy).then_inc(s("onT_ready"), 1)

            def evac_keys0(n, q):
                act.wait_ge(s("stT_ready"), n * 4 + 1)
                act.activation(keysT[q][:, 0:4, :], auxb[2].rearrange("p (j n) -> p j n", n=N), ACT.Copy)\
                   .then_inc(s("stack_read"), 1)

            def evac_keys1(n, q):
                act.wait_ge(s("stT_ready"), n * 4 + 2)
                act.activation(keysT[q][:, 4:8, :], auxb[1].rearrange("p (j n) -> p j n", n=N), ACT.Copy)\
                   .then_inc(s("keys1_read"), 1)

            def step(b, p):
                nxt, last = has_next(b), has_last(b)
                m, n = b - 1, b + 1
                exps(b, 0)
                exps(b, 1)
                if nxt:
                    evac_keys1(n, 1 - p)
                if last:
                    evac_pv(m, 1)
                exps(b, 2)
                if has_second(b):
                    evac_hT(b + 2)
                exps(b, 3)
                if has_second(b):
                    evac_qv(b + 2)
                exps(b, 4)
                exps(b, 5)
                evac_pv(b, 0)
                exps(b, 6)
                if last:
                    evac_onT(m)
                exps(b, 7)

            act.wait_ge(s("ident_ready"), 1)
            act.activation(warm[:, :], ident[:, 0:1], ACT.Exp)
            act.wait_ge(s("attn_weights"), 16 * 10)
            evac_hT(0)
            evac_qv(0)
            evac_hT(1)
            evac_keys0(0, 0)
            evac_qv(1)
            evac_keys1(0, 0)
            steps(act, None, 0, step)
            def norm_rows(u, which, dst, src, done):
                act.wait_ge(s(f"scale{which + 2}_ready"), u // 2 + 1)
                for k in range(UT * u, UT * u + UT):
                    i = act.activation(dst(k), src(k), ACT.Identity, bias=shift[:, which, k:k + 1],
                                       scale=rr[:, which, k:k + 1])
                i.then_inc(s(done), 1)

            def norm2(u):
                norm_rows(u, 0, lambda k: tn[:, k, :], lambda k: x1[:, k, :], "xn2_act")

            def norm3(u):
                norm_rows(u, 1, lambda k: rec[:, k, 0:D], lambda k: rec[:, k, D:2 * D], "tn_act")

            def copy_h2T(u):
                act.wait_ge(s("x2T_ready"), u + 1)
                act.activation(h2T[:, u, :], banks[2 * u][:, :], ACT.Identity, bias=cols[:, 3:4], scale=cols[:, 2:3])\
                   .then_inc(s("h2T_ready"), 1)

            def copy_qc(u):
                act.wait_ge(s("qc_ready"), u + 1)
                act.activation(qc[:, u, :], banks[2 * u + 1][:, :], ACT.Copy).then_inc(s("qc_copied"), 1)

            def exp_c(u):
                act.wait_ge(s("lg_ready"), u + 1)
                for k in (UB * u, UB * u + 1):
                    i = act.activation(at[:, k, :], lg[:, k, :], ACT.Exp, bias=nmx[:, k:k + 1],
                                       accum_out=ssum[:, k:k + 1])
                i.then_inc(s("at_ready"), 1)

            def copy_wp(u):
                act.wait_ge(s("wp_ready"), u + 1)
                act.activation(wp[:, UB * u:UB * u + UB, :].rearrange("p k d -> p (k d)"),
                               banks[2 * u + 1][:, 0:UB * D], ACT.Copy).then_inc(s("wp_copied"), 1)

            def copy_t(u):
                act.wait_ge(s("tTp_ready"), u + 1)
                act.activation(tT[:, u, :], banks[2 * u][:, :], ACT.Copy).then_inc(s("tT_ready"), 1)

            def exp_r(g):
                act.wait_ge(s("rmx_ready"), g + 1)
                act.activation(re[:, GT * g:GT * g + GT, :], rl[:, GT * g:GT * g + GT, :], ACT.Exp)\
                   .then_inc(s("re_ready"), 1)

            norm2(1)
            evac_pv(B - 1, 1)
            copy_h2T(0)
            copy_h2T(1)
            evac_onT(B - 1)
            copy_qc(0)
            copy_qc(1)
            norm2(3)
            copy_h2T(2)
            exp_c(0)
            copy_h2T(3)
            exp_c(1)
            copy_wp(0)
            copy_qc(2)
            copy_wp(1)
            copy_qc(3)
            exp_c(2)
            exp_c(3)
            copy_wp(2)
            copy_wp(3)
            norm3(1)
            copy_t(0)
            copy_t(1)
            norm3(3)
            copy_t(2)
            exp_r(0)
            copy_t(3)
            exp_r(1)
            pad_rows(act, E // 2, E)
            act.activation(warm[:, :], ident[:, 0:1], ACT.Gelu_apprx_tanh)

            def copy_tT(j, k):
                act.wait_ge(s("tj_ready"), j + 1)
                ge(act, s("h_ready"), j - 1)
                act.activation(tTj[k % 2][:, :], banks[k % 2][:, 0:P], ACT.Copy).then_inc(s("tTj_ready"), 1)

            def gelu(j, k):
                act.wait_ge(s("hpre_ready"), j + 1)
                ge(act, s("z_ready"), j - 1)
                act.activation(hj[k % 2][:, :, :], hpre[k % 2][:, :, :], ACT.Gelu_apprx_tanh)\
                   .then_inc(s("gelu_ready"), 1)

            def copy_w1(j, k):
                ex = act.value_load(col_at(etab, j), min_val=0, max_val=E - 1)
                ge(act, s("h_ready"), j - RING + 1)
                act.activation(w1j[k][:, :], w1s[:, bass.ds(ex, 1), :].rearrange("p e f -> p (e f)"), ACT.Copy)\
                   .then_inc(s("w1_copied"), 1)

            act.wait_ge(s("table_ready"), 1)
            act.wait_ge(s("moe_weights"), 4 * 16)
            copy_w1(0, 0)
            copy_w1(1, 1)
            copy_w1(2, 2)
            copy_tT(0, 0)
            copy_tT(1, 1)
            gelu(0, 0)

            def step(j, k, turn):
                if ahead(j, 2):
                    copy_tT(j + 2, k)
                if ahead(j, 1):
                    gelu(j + 1, k + 1)
                if ahead(j, 3):
                    copy_w1(j + 3, (k + 3) % RING)

            tiles_of_experts(act, step)

        @block.vector
        def _(dve):
            link = Link(dve, s("dve_link"))

            def seed_of_both(a, b_):
                k = slice(a, b_)
                dve.tensor_scalar(ve[:, 0, k], mv[:, k, 1], EPS, None, ALU.add)
                link(dve.tensor_scalar(ve[:, 1, k], mv[:, k, 1], 1.0 + EPS, EPS * EPS, ALU.mult, ALU.add))
                link(dve.tensor_scalar(ri[:, :, k], ve[:, :, k].bitcast(I32), 1, None, ALU.arith_shift_right))
                dve.tensor_scalar(ri[:, :, k], ri[:, :, k], -1.0, MAGIC, ALU.mult, ALU.add)\
                   .then_inc(s("rest_seeded"), 1)

            def newton(dst, v, seed, half):
                link(dve.tensor_scalar(seed, v.bitcast(I32), 1, None, ALU.arith_shift_right))
                link(dve.tensor_scalar(seed, seed, -1.0, MAGIC, ALU.mult, ALU.add))
                g = seed.bitcast(F32)
                for step in range(3):
                    link(dve.tensor_tensor(half, g, g, ALU.mult))
                    link(dve.scalar_tensor_tensor(half, half, -0.5, v, ALU.mult, ALU.mult))
                    link(dve.scalar_tensor_tensor(dst, half, 1.5, g, ALU.add, ALU.mult))
                    g = dst

            def bn(src, a, b_):
                for t in range(a, b_):
                    c = link.mark(dve.bn_stats(bn6[:, t, :], src[:, t, :]))
                link.wait(c)
                for t in range(a, b_):
                    c = link.mark(dve.bn_aggr(mv[:, t, :], bn6[:, t, :]))
                link.wait(c)

            def seed_of_tn(a, b_):
                k = slice(a, b_)
                link.wait(link.n)
                link(dve.tensor_scalar(ve[:, 1, k], mv[:, k, 1], EPS, None, ALU.add))
                link(dve.tensor_scalar(ri[:, 1, k], ve[:, 1, k].bitcast(I32), 1, None, ALU.arith_shift_right))
                dve.tensor_scalar(ri[:, 1, k], ri[:, 1, k], -1.0, MAGIC, ALU.mult, ALU.add)\
                   .then_inc(s("tn_seeded"), 1)

            def shift_of_tn(a, b_):
                k = slice(a, b_)
                dve.wait_ge(s("tn_scaled"), 1)
                dve.scalar_tensor_tensor(shift[:, 1, k], mv[:, k, 0], -1.0, rr[:, 1, k], ALU.mult,
                                         ALU.mult).then_inc(s("scale3_ready"), 1)

            def scale_and_shift(which, stats, a, b_):
                k = slice(a, b_)
                link.wait(link.n)
                link(dve.tensor_scalar(ve[:, which, k], stats[:, k, 1], EPS, None, ALU.add))
                newton(rr[:, which, k], ve[:, which, k], ri[:, which, k], rt[:, which, k])
                dve.scalar_tensor_tensor(shift[:, which, k], stats[:, k, 0], -1.0, rr[:, which, k], ALU.mult,
                                         ALU.mult).then_inc(s(f"scale{which + 2}_ready"), 1)

            def rsqrt_of_both(a, b_):
                k = slice(a, b_)
                dve.tensor_scalar(ve[:, 0, k], mv[:, k, 1], EPS, None, ALU.add)
                link(dve.tensor_scalar(ve[:, 1, k], mv[:, k, 1], 1.0 + EPS, EPS * EPS, ALU.mult, ALU.add))
                newton(rr[:, :, k], ve[:, :, k], ri[:, :, k], rt[:, :, k])
                link(dve.tensor_tensor(rt[:, 0, k], rr[:, 0, k], ve[:, 0, k], ALU.mult))
                link(dve.tensor_tensor(rr[:, 1, k], rr[:, 1, k], rt[:, 0, k], ALU.mult))

            def normalise(n):
                ge(dve, s("xT_ready"), n)
                for t in range(T):
                    c = link.mark(dve.tensor_scalar(x0[:, n * T + t, :], xin[:, n * T + t, :], mv[:, n * T + t, 0:1],
                                                    r1_at(n, t), ALU.subtract, ALU.mult))
                link.wait(c)
                for t in range(T):
                    i = dve.tensor_scalar(xh[:, t, :], x0[:, n * T + t, :], r2_at(n, t), None, ALU.mult)
                i.then_inc(s("xn_ready"), 1)

            def r1_at(n, t):
                return rr[:, 0, n * T + t:n * T + t + 1] if isinstance(n, int) else rr[:, 0, bass.ds(n * T + t, 1)]

            def r2_at(n, t):
                return rr[:, 1, n * T + t:n * T + t + 1] if isinstance(n, int) else rr[:, 1, bass.ds(n * T + t, 1)]

            q8 = qs[:, :, :].rearrange("p t (h d) -> p (t h) d", d=DH)

            def pieces(n, between=None):
                dve.wait_ge(s("q_ready"), n + 1)
                ge(dve, s("stT_ready"), n * 4)
                a0 = link.mark(dve.tensor_copy(stackA[:, :, 0:8], q8))
                b0 = link.mark(dve.tensor_tensor(pf[:, :, :].rearrange("p (t h) d -> p t (h d)", t=T), qs[:, :, :],
                                                 s2b[:, :, :].rearrange("p h d -> p (h d)").unsqueeze(1)
                                                 .broadcast_to([P, T, D]), ALU.mult))
                link.wait(a0)
                a1 = link.mark(dve.tensor_tensor(ra[:, :, :], q8, stackA[:, :, 0:8], ALU.subtract))
                link.wait(b0)
                b1 = link.mark(dve.tensor_copy(stackB[:, :, 0:8], pf[:, :, :]))
                dve.wait_ge(s("sq_ready"), n + 1)
                c = link.mark(dve.reduce_sum(c0[:, :], sq[:, :, :].rearrange("p t (h d) -> p (t h) d", d=DH), AX_X))
                link.wait(a1)
                a2 = link.mark(dve.tensor_copy(stackA[:, :, 24:32], ra[:, :, :]))
                link.wait(c)
                dve.tensor_tensor(cf[:, :], c0[:, :], snegb[:, :, :].rearrange("p t h -> p (t h)"),
                                  ALU.mult).then_inc(s("sum_ready"), 1)
                b2_ = link.mark(dve.tensor_tensor(rb[:, :, :], pf[:, :, :], stackB[:, :, 0:8], ALU.subtract))
                link.wait(a2)
                dve.tensor_tensor(stackA[:, :, 40:48], ra[:, :, :], stackA[:, :, 24:32], ALU.subtract)
                dve.tensor_copy(stackA[:, :, 8:24].rearrange("p k (r d) -> p k r d", d=8),
                                stackA[:, :, 0:8].unsqueeze(2).broadcast_to([P, T * H, 2, 8]))
                dve.tensor_copy(stackA[:, :, 32:40], stackA[:, :, 24:32]).then_inc(s("keys_ready"), 1)
                if between:
                    between()
                link.wait(b2_)
                link(dve.tensor_copy(stackB[:, :, 8:16], rb[:, :, :]))
                dve.tensor_tensor(stackB[:, :, 16:24], rb[:, :, :], stackB[:, :, 8:16], ALU.subtract)
                dve.tensor_copy(stackB[:, :, 24:40], stackB[:, :, 0:16])
                dve.tensor_copy(stackB[:, :, 40:48], stackB[:, :, 0:8]).then_inc(s("qrys_ready"), 1)

            def evac_stack(n, q, k):
                bank = auxb[(2, 1, 2, 1)[k]].rearrange("p (j n) -> p j n", n=N)
                dve.wait_ge(s("stT_ready"), n * 4 + k + 1)
                pr = slice(4 * (k % 2), 4 * (k % 2) + 4)
                if k == 0:
                    dve.tensor_copy(keysT[q][:, pr, :], bank).then_inc(s("stack_read"), 1)
                else:
                    dve.tensor_copy(qrysT[q][0:64, pr, 0, :], bank[0:64])
                    dve.tensor_copy(qrysT[q][64:128, pr, 1, :], bank[64:128]).then_inc(s("stack_read"), 1)

            def divide(m, half):
                bank = aux[1 - half][:, :].rearrange("p (t k c) -> p t k c", t=T, c=32)
                dve.wait_ge(s("oT_ready"), m * 2 + 2 - half)
                hd = slice(8 * half, 8 * half + 8)
                link(dve.reciprocal(rden[:, :, hd], bank[:, :, :, DH]))
                dve.tensor_tensor(on[:, :, hd, :], bank[:, :, :, 0:DH],
                                  rden[:, :, hd].unsqueeze(3).broadcast_to([P, T, 8, DH]),
                                  ALU.mult).then_inc(s("on_ready"), 1)

            def residual1(m):
                dve.wait_ge(s("proj_ready"), m + 1)
                dve.tensor_tensor(tiles(x1, m), aux[0][:, 0:N].rearrange("p (t d) -> p t d", t=T), tiles(x0, m),
                                  ALU.add).then_inc(s("x1_ready"), 1)

            def norm2(u):
                for k in range(UT * u, UT * u + UT):
                    i = dve.tensor_scalar(tn[:, k, :], x1[:, k, :], mvB[:, k, 0:1], rr[:, 0, k:k + 1], ALU.subtract,
                                          ALU.mult)
                i.then_inc(s("xn2_dve"), 1)

            def stats1(m):
                dve.wait_ge(s("x1_ready"), m + 1)
                for t in range(T):
                    c = link.mark(dve.bn_stats(bn6[:, m * T + t, :], x1[:, m * T + t, :]))
                link.wait(c)
                for t in range(T):
                    link.mark(dve.bn_aggr(mvB[:, m * T + t, :], bn6[:, m * T + t, :]))

            def tiles(x, m):
                return x[:, m * T:m * T + T, :] if isinstance(m, int) else x[:, bass.ds(m * T, T), :]

            def step(b, p):
                nxt, last = has_next(b), has_last(b)
                if nxt:
                    evac_stack(b + 1, 1 - p, 0)
                if isinstance(b, int) and b == 0:
                    dve.wait_ge(s("rest_scaled"), 1)
                if has_second(b):
                    normalise(b + 2)
                if nxt:
                    evac_stack(b + 1, 1 - p, 2)
                    evac_stack(b + 1, 1 - p, 3)
                if isinstance(b, int) and b == B - 1:
                    scale_and_shift(0, mvB, 0, GT)
                    dve.wait_ge(s("scale2_ready"), 1)
                    norm2(0)
                    stats1(B - 4)
                    stats1(B - 3)
                if last:
                    divide(b - 1, 1)
                    divide(b - 1, 0)
                if has_second(b):
                    pieces(b + 2)
                if last:
                    residual1(b - 1)
                if isinstance(b, int) and b == B - 2:
                    for k in range(B // 2):
                        stats1(k)
                if isinstance(b, int) and b == B - 1:
                    stats1(B - 2)

            dve.wait_ge(s("x_first"), 16)
            bn(xin, 0, 2 * T)
            rsqrt_of_both(0, 2 * T)
            normalise(0)
            for buf in (stackA, stackB):
                c = link.mark(dve.memset(buf[:, :, SUMCOL:SLOT], 0.0))
            link.wait(c)
            dve.memset(stackA[:, :, SUMCOL + 3:SUMCOL + 9], 1.0)
            dve.memset(stackB[:, :, SUMCOL:SUMCOL + 3], 1.0).then_inc(s("consts_ready"), 1)
            dve.wait_ge(s("attn_weights"), 16 * 10)
            SCALE = float(DH) ** -0.5
            dve.tensor_scalar(s2b[:, :, :], taub[:, :].unsqueeze(2).broadcast_to([P, H, DH]), 2.0 * SCALE, None,
                              ALU.mult)
            for t in range(T):
                c = link.mark(dve.tensor_scalar(snegb[:, t, :], taub[:, :], -SCALE, None, ALU.mult))
            normalise(1)
            link.wait(c)
            dve.wait_ge(s("x_rest"), 16)
            bn(xin, 2 * T, 5 * T)
            pieces(0)
            bn(xin, 5 * T, TILES)
            seed_of_both(2 * T, TILES)
            dve.wait_ge(s("zeros_ready"), 4)
            for k in (2, 3):
                evac_stack(0, 0, k)
            pieces(1)
            dve.memset(oh[:, 0, :], 0.0)
            link(dve.tensor_tensor(wog_t[:, :], wog_t[:, :], g1b[:, :], ALU.mult))
            steps(dve, link, 2 * 12, step)
            m = B - 1
            divide(m, 1)
            divide(m, 0)
            residual1(m)
            stats1(m)
            link.wait(link.n)

            dve.wait_ge(s("chan_weights"), 16 * 6)
            dve.tensor_scalar(cols[:, 5:6], cols[:, 4:5], 2.0 / N ** 0.5, None, ALU.mult)
            dve.tensor_tensor(wogc[:, :], wogc[:, :], g2b[:, :], ALU.mult)
            dve.wait_ge(s("consts_ready"), 9)
            link(dve.tensor_scalar(minus8[:, :], iota8[:, :], float(E), None, ALU.subtract))

            def batches(x, u):
                return x[:, UB * u:UB * u + UB]

            def mask_and_max(u):
                dve.wait_ge(s("gram_ready"), u + 1)
                link(dve.scalar_tensor_tensor(batches(lg, u)[:, :, :],
                                              banks[2 * u][:, 0:UB * D].rearrange("p (k d) -> p k d", d=D),
                                              cols[:, 5:6], mask[:, :].unsqueeze(1).broadcast_to([P, UB, D]),
                                              ALU.mult, ALU.add))
                dve.tensor_reduce(batches(nmx, u), batches(lg, u)[:, :, :], AX_X, ALU.max, negate=True)\
                   .then_inc(s("lg_ready"), 1)

            def over_sum(u):
                dve.wait_ge(s("at_ready"), u + 1)
                link(dve.reciprocal(batches(rsum, u), batches(ssum, u)))
                dve.tensor_tensor(batches(atn, u)[:, :, :], batches(at, u)[:, :, :],
                                  batches(rsum, u).unsqueeze(2).broadcast_to([P, UB, D]), ALU.mult)\
                   .then_inc(s("atn_ready"), 1)

            def copy_wpp(u):
                dve.wait_ge(s("wpp_ready"), u + 1)
                dve.tensor_copy(batches(wpp, u)[:, :, :].rearrange("p k d -> p (k d)"), banks[2 * u][:, 0:UB * D])\
                   .then_inc(s("wpp_copied"), 1)

            def result(u):
                if u % 2 == 0:
                    dve.wait_ge(s("scaled_ready"), u // 2 + 1)
                dve.wait_ge(s("x2_ready"), u + 1)
                k = slice(UT * u, UT * u + UT)
                dve.tensor_tensor(rec[:, k, D:2 * D], banks[2 * u + 1][:, :].rearrange("p (t d) -> p t d", d=D),
                                  xin[:, k, :], ALU.add).then_inc(s("y_ready"), 1)

            def stats3(u):
                dve.wait_ge(s("y_ready"), u + 1)
                bn(rec[:, :, D:2 * D], UT * u, UT * u + UT)

            def norm3(u):
                for k in range(UT * u, UT * u + UT):
                    i = dve.tensor_scalar(rec[:, k, 0:D], rec[:, k, D:2 * D], mv[:, k, 0:1], rr[:, 1, k:k + 1],
                                          ALU.subtract, ALU.mult)
                i.then_inc(s("tn_dve"), 1)

            over_e = lambda x: x.unsqueeze(2).broadcast_to([P, GT, E])
            over_t = lambda x: x[:, :].unsqueeze(1).broadcast_to([P, GT, E])

            def route(g):
                a, k = GT * g, slice(GT * g, GT * g + GT)
                dve.wait_ge(s("rl_ready"), g + 1)
                link(dve.tensor_tensor(rl[:, k, :], banks[4 * g + 1][:, 0:GT * E].rearrange("p (t e) -> p t e", e=E),
                                       swb[:, :].unsqueeze(1).broadcast_to([P, GT, E]), ALU.add))
                link(dve.tensor_reduce(rmx[:, k], rl[:, k, :], AX_X, ALU.max))
                dve.tensor_tensor(rl[:, k, :], rl[:, k, :], over_e(rmx[:, k]), ALU.subtract)\
                   .then_inc(s("rmx_ready"), 1)

            def choose(g):
                a, k = GT * g, slice(GT * g, GT * g + GT)
                dve.wait_ge(s("re_ready"), g + 1)
                link(dve.tensor_reduce(rmx[:, k], re[:, k, :], AX_X, ALU.max))
                link(dve.tensor_tensor(cand[:, :, :], re[:, k, :], over_e(rmx[:, k]), ALU.is_equal))
                link(dve.tensor_tensor(cand[:, :, :], cand[:, :, :], over_t(minus8), ALU.mult))
                link(dve.tensor_reduce(first[:, :], cand[:, :, :], AX_X, ALU.min))
                dve.tensor_tensor(oh[:, a + 1:a + GT + 1, :], over_e(first[:, :]), over_t(minus8), ALU.is_equal)\
                   .then_inc(s("oh_ready"), 1)
                link(dve.reduce_sum(rs[:, :], re[:, k, :], AX_X))
                link(dve.reciprocal(rs[:, :], rs[:, :]))
                link(dve.tensor_tensor(rec[:, k, PROB], rs[:, :], rmx[:, k], ALU.mult))

            def place(g):
                a = GT * g
                dve.wait_ge(s("rank_ready"), g + 1)
                link(dve.tensor_tensor(rank[:, :, :], banks[4 * g + 3][:, 0:GT * E].rearrange("p (t e) -> p t e", e=E),
                                       over_t(ebase), ALU.add))
                link(dve.tensor_tensor(rank[:, :, :], rank[:, :, :], oh[:, a + 1:a + GT + 1, :], ALU.mult))
                link(dve.reduce_sum(first[:, :], rank[:, :, :], AX_X))
                dve.tensor_copy(pos[:, a:a + GT], first[:, :]).then_inc(s("pos_ready"), 1)

            scale_and_shift(0, mvB, GT, TILES)
            dve.wait_ge(s("scale2_ready"), 2)
            norm2(2)
            mask_and_max(0)
            mask_and_max(1)
            over_sum(0)
            over_sum(1)
            copy_wpp(0)
            mask_and_max(2)
            result(0)
            copy_wpp(1)
            stats3(0)
            mask_and_max(3)
            over_sum(2)
            result(1)
            over_sum(3)
            stats3(1)
            seed_of_tn(0, GT)
            copy_wpp(2)
            copy_wpp(3)
            result(2)
            stats3(2)
            shift_of_tn(0, GT)
            norm3(0)
            result(3)
            stats3(3)
            scale_and_shift(1, mv, GT, TILES)
            dve.wait_ge(s("scale3_ready"), 2)
            norm3(2)
            route(0)
            choose(0)
            place(0)
            route(1)
            choose(1)
            place(1)
            count = banks[4][:, 0:E]
            over_j = lambda x: x[:, :].unsqueeze(1).broadcast_to([P, JT, E])
            link(dve.tensor_scalar(cnt_i[:, :], count, float(P - 1), None, ALU.add))
            dve.tensor_tensor(ptab[:, :], count, ebase[:, :], ALU.add).then_inc(s("pads_placed"), 1)
            link(dve.tensor_scalar(cnt_i[:, :], cnt_i[:, :], P.bit_length() - 1, None, ALU.arith_shift_right))
            link(dve.tensor_copy(ntile[:, :], cnt_i[:, :]))
            link(dve.tensor_tensor_scan(cum[:, :], ones8[:, :], ntile[:, :], 0.0, ALU.mult, ALU.add))
            link(dve.tensor_tensor(past[:, :, :], jiota[:, :].unsqueeze(2).broadcast_to([P, JT, E]), over_j(cum),
                                   ALU.is_ge))
            link(dve.reduce_sum(ej[:, :], past[:, :, :], AX_X))
            link(dve.tensor_tensor(past[:, :, :], past[:, :, :], over_j(ntile), ALU.mult))
            link(dve.reduce_sum(rj[:, :], past[:, :, :], AX_X))
            link(dve.tensor_tensor(rj[:, :], jiota[:, :], rj[:, :], ALU.subtract))
            link(dve.tensor_scalar(rj[:, :], rj[:, :], float(P), None, ALU.mult))
            link(dve.scalar_tensor_tensor(rj[:, :], ej[:, :], float(REGION), rj[:, :], ALU.mult, ALU.add))
            link(dve.tensor_scalar(rtab[:, :], rj[:, :], float(E * REGION), None, ALU.min))
            dve.tensor_scalar(etab[:, :], ej[:, :], float(E - 1), None, ALU.min).then_inc(s("table_ready"), 1)

            dve.wait_ge(s("moe_weights"), 4 * 16)
            dve.wait_ge(s("table_ready"), 1)
            link(dve.tensor_tensor(past[:, :, :], ej[:, :].unsqueeze(2).broadcast_to([P, JT, E]), over_j(iota8),
                                   ALU.is_equal))
            link(dve.tensor_tensor(b1e[:, :, :, :], past[:, :, :].unsqueeze(2).broadcast_to([P, JT, FT, E]),
                                   b1s[:, :, :].rearrange("p e f -> p f e").unsqueeze(1)
                                   .broadcast_to([P, JT, FT, E]), ALU.mult))
            link(dve.reduce_sum(b1j[:, :, :], b1e[:, :, :, :], AX_X))

            def add_b1(j, k):
                dve.wait_ge(s("h_ready"), j + 1)
                ge(dve, s("gelu_ready"), j - 1)
                dve.tensor_tensor(hpre[k % 2][:, :, :], banks[2 + k % 2][:, :].rearrange("p (f t) -> p f t", f=FT),
                                  at_j(b1j, j).unsqueeze(2)
                                  .broadcast_to([P, FT, P]), ALU.add).then_inc(s("hpre_ready"), 1)

            def finish(j, k, turn):
                ex = dve.value_load(col_at(etab, j), min_val=0, max_val=E - 1)
                dve.wait_ge(s("z_ready"), j + 1)
                dve.tensor_tensor(zj[k % 2][:, :], banks[4 + k % 2][:, 0:D],
                                  b2b[:, bass.ds(ex, 1), :].rearrange("p e d -> p (e d)"), ALU.add)\
                   .then_inc(s("zj_ready"), 1)
                dve.wait_ge(s("zj_ready"), j + 1)
                dve.scalar_tensor_tensor(at_j(oj, j), zj[k % 2][:, :], at_j(recj, j)[:, PROB:PROB + 1],
                                         at_j(recj, j)[:, D:2 * D],
                                         ALU.mult, ALU.add).then_inc(s("o_ready"), 1)

            def copy_tokens(j, k, turn):
                dve.wait_ge(s(f"rec_loaded{k}"), turn * 16 + 16)
                ge(dve, s("tj_ready"), j - 1)
                dve.tensor_copy(tj[k % 2][:, :], at_j(recj, j)[:, 0:D]).then_inc(s("tj_copied"), 1)

            for k in range(3):
                copy_tokens(k, k, 0)
            add_b1(0, 0)

            def step(j, k, turn):
                if ahead(j, 3):
                    copy_tokens(j + 3, (k + 3) % RING, turn + (k + 3) // RING)
                if ahead(j, 1):
                    add_b1(j + 1, k + 1)
                finish(j, k, turn)

            tiles_of_experts(dve, step)

        @block.tensor
        def _(pe):
            def normT(n):
                pe.wait_ge(s("xn_ready"), n + 1)
                for t in range(T):
                    i = pe.transpose(aux[0][:, t * P:t * P + P], xh[:, t, :], ident[:, :])
                i.then_inc(s("xT_ready"), 1)

            def project_qv(n):
                pe.wait_ge(s("hT_ready"), n + 1)
                bank = qv_bank(n)
                if bank is aux[2]:
                    ge(pe, s("stack_read"), n * 3 - 1)
                for t in range(T):
                    i = pe.matmul(bank[:, t * 2 * D:(t + 1) * 2 * D], hT[:, t * P:t * P + P], wqkv[:, :],
                                  start=True, stop=True)
                i.then_inc(s("qv_ready"), 1)

            def stackT(n, k):
                if k == 0:
                    pe.wait_ge(s("keys_ready"), n + 1)
                    pe.wait_ge(s("sums_ready"), n * 2 + 1)
                    pe.wait_ge(s("vs_ready"), n + 1)
                if k == 2:
                    pe.wait_ge(s("qrys_ready"), n + 1)
                    pe.wait_ge(s("sums_ready"), n * 2 + 2)
                    pe.wait_ge(s("stack_read"), n * 3 + 1)
                if k == 3:
                    pe.wait_ge(s("keys1_read"), n + 1)
                bank = auxb[(2, 1, 2, 1)[k]]
                src = stackA if k < 2 else stackB
                for jj in range(4):
                    j = 4 * (k % 2) + jj
                    for t in range(T):
                        h = t * H + 2 * j
                        i = pe.transpose(bank[:, jj * N + t * P:jj * N + t * P + P],
                                         src[:, h:h + 2, :].rearrange("p h c -> p (h c)"), identb[:, :])
                i.then_inc(s("stT_ready"), 1)

            def logits(b, p, j):
                if j == 0:
                    pe.wait_ge(s("stack_read"), b * 3 + 3)
                    pe.wait_ge(s("keys1_read"), b + 1)
                ge(pe, s("exp_ready"), b * 8 + j - 1)
                for t in range(T):
                    i = pe.matmul(logit_banks[j % 2][t][:, :], keysT[p][:, j, t * P:t * P + P],
                                  qrysT[p][:, j, :, :].rearrange("p e n -> p (e n)"), start=True, stop=True)
                i.then_inc(s("logits_ready"), 1)

            def pv(b, p, g):
                pe.wait_ge(s("exp_ready"), b * 8 + 2 * g + 2)
                if g == 0:
                    pe.wait_ge(s("v_ready"), b + 1)
                if g % 2 == 0:
                    ge(pe, s("o_read"), b * 2 + g // 2)
                for t in range(T):
                    for jj in range(4):
                        i = pe.matmul(pv_bank[32 * jj:32 * jj + 32, (g % 2) * N:(g % 2) * N + N],
                                      vaug[p][:, t, 4 * g + jj, :], expo[(2 * g + jj // 2) % 4][:, t, jj % 2, :],
                                      start=(t == 0), stop=(t == T - 1))
                i.then_inc(s("pv_done"), 1)

            def oT_back(m, half):
                pe.wait_ge(s("o_read"), m * 2 + half + 1)
                if half == 0:
                    pe.wait_ge(s("stack_read"), min(m + 3, B) * 3 if isinstance(m, int) else m * 3 + 9)
                elif isinstance(m, int):
                    ge(pe, s("x1_ready"), m)
                for t in range(T):
                    for gg in range(2):
                        i = pe.transpose(aux[1 - half][:, (t * 2 + gg) * P:(t * 2 + gg) * P + P],
                                         oT[:, 2 * half + gg, t * P:t * P + P], ident[:, :])
                i.then_inc(s("oT_ready"), 1)

            def onT_(m):
                pe.wait_ge(s("on_ready"), m * 2 + 2)
                for t in range(T):
                    i = pe.transpose(aux[1][:, t * P:t * P + P], on[:, t, :, :].rearrange("p h d -> p (h d)"),
                                     ident[:, :])
                i.then_inc(s("onTp_ready"), 1)

            def project_o(m):
                pe.wait_ge(s("onT_ready"), m + 1)
                for t in range(T):
                    i = pe.matmul(aux[0][:, t * D:t * D + D], onT[:, t * P:t * P + P], wog_t[:, :], start=True,
                                  stop=True)
                i.then_inc(s("proj_ready"), 1)

            def step(b, p):
                nxt, last = has_next(b), has_last(b)
                m, n = b - 1, b + 1
                logits(b, p, 0)
                logits(b, p, 1)
                if nxt:
                    stackT(n, 0)
                    stackT(n, 1)
                if last:
                    pv(m, 1 - p, 3)
                logits(b, p, 2)
                if nxt:
                    stackT(n, 2)
                if has_second(b):
                    normT(b + 2)
                logits(b, p, 3)
                pv(b, p, 0)
                if nxt:
                    stackT(n, 3)
                if has_second(b):
                    project_qv(b + 2)
                logits(b, p, 4)
                if last:
                    oT_back(m, 1)
                logits(b, p, 5)
                if last:
                    oT_back(m, 0)
                pv(b, p, 1)
                logits(b, p, 6)
                logits(b, p, 7)
                if last:
                    onT_(m)
                pv(b, p, 2)
                if last:
                    project_o(m)

            pe.wait_ge(s("ident_ready"), 2)
            pe.wait_ge(s("attn_weights"), 16 * 10)
            normT(0)
            project_qv(0)
            normT(1)
            project_qv(1)
            for k in range(4):
                stackT(0, k)
            pe.wait_ge(s("vs_ready"), 2)
            steps(pe, None, 0, step)
            pe.wait_ge(s("chan_weights"), 16 * 6)
            pe.wait_ge(s("consts_ready"), 9)

            def from_rows(u, by_dve, by_act, src, done):
                pe.wait_ge(s(by_act if u % 2 else by_dve), u // 2 + 1)
                for t in range(UT):
                    i = pe.transpose(banks[2 * u][:, t * P:t * P + P], src(UT * u + t), ident[:, :])
                i.then_inc(s(done), 1)

            def x2T(u):
                from_rows(u, "xn2_dve", "xn2_act", lambda k: tn[:, k, :], "x2T_ready")

            def tTp(u):
                from_rows(u, "tn_dve", "tn_act", lambda k: rec[:, k, 0:D], "tTp_ready")

            def project_c(u):
                pe.wait_ge(s("h2T_ready"), u + 1)
                for t in range(UT):
                    i = pe.matmul(banks[2 * u + 1][:, t * D:t * D + D], h2T[:, u, t * P:t * P + P], wqkc[:, :],
                                  start=True, stop=True)
                i.then_inc(s("qc_ready"), 1)

            def gram(u):
                pe.wait_ge(s("qc_copied"), u + 1)
                for k in range(UB):
                    o = banks[2 * u][:, k * D:k * D + D]
                    at_t = lambda t: slice((k * T + t) * D, (k * T + t) * D + D)
                    for t in range(T):
                        pe.matmul(o, qc[:, u, at_t(t)], qc[:, u, at_t(t)], start=(t == 0), stop=False)
                    if k == 0:
                        pe.wait_ge(s("sqc_ready"), u + 1)
                    for t in range(T):
                        pe.matmul(o, nhalf[:, :], sqc[:, u, at_t(t)], start=False, stop=False)
                        i = pe.matmul(o, sqc[:, u, at_t(t)], nhalf[:, :], start=False, stop=(t == T - 1))
                i.then_inc(s("gram_ready"), 1)

            def attn_wo(u):
                pe.wait_ge(s("atn_ready"), u + 1)
                for k in range(UB):
                    i = pe.matmul(banks[2 * u + 1][:, k * D:k * D + D], atn[:, UB * u + k, :], wogc[:, :], start=True,
                                  stop=True)
                i.then_inc(s("wp_ready"), 1)

            def wv_attn_wo(u):
                pe.wait_ge(s("wp_copied"), u + 1)
                for k in range(UB):
                    i = pe.matmul(banks[2 * u][:, k * D:k * D + D], wvTc[:, :], wp[:, UB * u + k, :], start=True,
                                  stop=True)
                i.then_inc(s("wpp_ready"), 1)

            def apply_c(u):
                pe.wait_ge(s("wpp_copied"), u + 1)
                for t in range(UT):
                    i = pe.matmul(banks[2 * u + 1][:, t * D:t * D + D], h2T[:, u, t * P:t * P + P],
                                  wpp[:, UB * u + t // T, :], start=True, stop=True)
                i.then_inc(s("x2_ready"), 1)

            def router(g):
                for u in (2 * g, 2 * g + 1):
                    pe.wait_ge(s("tT_ready"), u + 1)
                    for t in range(UT):
                        c = ((u % 2) * UT + t) * E
                        i = pe.matmul(banks[4 * g + 1][:, c:c + E], tT[:, u, t * P:t * P + P], sww[:, :], start=True,
                                      stop=True)
                i.then_inc(s("rl_ready"), 1)

            def ranks(g):
                pe.wait_ge(s("oh_ready"), g + 1)
                a = GT * g
                bank = banks[4 * g + 3]
                oh2 = lambda u, v: oh[:, u + 1:v + 1, :].rearrange("p t e -> p (t e)")
                for back in range(1, a + GT):
                    u = max(back, a) if back > 1 else a
                    pe.matmul(bank[:, (u - a) * E:GT * E], onesb[:, :], oh2(u - back, a + GT - back),
                              start=(back == 1), stop=False, skip_group_check=True)
                i = pe.matmul(bank[:, 0:GT * E], before[:, :], oh2(a, a + GT), start=False, stop=True,
                              skip_group_check=True)
                if g == 1:
                    for k in range(TILES):
                        i = pe.matmul(banks[4][:, 0:E], onesb[:, :], oh2(k, k + 1), start=(k == 0),
                                      stop=(k == TILES - 1))
                i.then_inc(s("rank_ready"), 1)

            m = B - 1
            pv(m, 1, 3)
            pe.wait_ge(s("exp_ready"), B * 8)
            x2T(0)
            x2T(1)
            oT_back(m, 1)
            oT_back(m, 0)
            project_c(0)
            onT_(m)
            project_c(1)
            project_o(m)
            gram(0)
            gram(1)
            pe.wait_ge(s("x1_ready"), B)
            x2T(2)
            x2T(3)
            attn_wo(0)
            project_c(2)
            attn_wo(1)
            wv_attn_wo(0)
            project_c(3)
            gram(2)
            apply_c(0)
            wv_attn_wo(1)
            gram(3)
            apply_c(1)
            attn_wo(2)
            wv_attn_wo(2)
            attn_wo(3)
            wv_attn_wo(3)
            apply_c(2)
            apply_c(3)
            tTp(0)
            tTp(1)
            router(0)
            tTp(2)
            tTp(3)
            ranks(0)
            router(1)
            ranks(1)
            
            def tokensT(j, k, turn):
                pe.wait_ge(s("tj_copied"), j + 1)
                pe.transpose(banks[k % 2][:, 0:P], tj[k % 2][:, :], ident[:, :]).then_inc(s("tj_ready"), 1)

            def layer1(j, k, turn):
                pe.wait_ge(s("w1_copied"), j + 1)
                pe.wait_ge(s("tTj_ready"), j + 1)
                ge(pe, s("hpre_ready"), j - 1)
                for f in range(FT):
                    i = pe.matmul(banks[2 + k % 2][:, f * P:f * P + P], w1j[k][:, f * P:f * P + P], tTj[k % 2][:, :],
                                  start=True, stop=True)
                i.then_inc(s("h_ready"), 1)

            def layer2(j, k):
                ex = pe.value_load(col_at(etab, j), min_val=0, max_val=E - 1)
                pe.wait_ge(s("gelu_ready"), j + 1)
                ge(pe, s("o_ready"), j - 1)
                for f in range(FT):
                    i = pe.matmul(banks[4 + k % 2][:, 0:D], hj[k % 2][:, f, :],
                                  w2s[:, bass.ds(ex, 1), f, :].rearrange("p e d -> p (e d)"), start=(f == 0),
                                  stop=(f == FT - 1))
                i.then_inc(s("z_ready"), 1)

            pe.wait_ge(s("table_ready"), 1)
            pe.wait_ge(s("moe_weights"), 4 * 16)
            tokensT(0, 0, 0)
            tokensT(1, 1, 0)
            layer1(0, 0, 0)

            def step(j, k, turn):
                if ahead(j, 2):
                    tokensT(j + 2, (k + 2) % RING, turn + (k + 2) // RING)
                if ahead(j, 1):
                    layer1(j + 1, (k + 1) % RING, turn + (k + 1) // RING)
                layer2(j, k)

            tiles_of_experts(pe, step)


def kernel(**inputs):
    import numpy as _np
    import concourse.bacc as _bacc
    from concourse import mybir as _mybir
    from concourse.bass_utils import run_bass_kernel_spmd as _run

    a = {k.split("_", 2)[2]: _np.asarray(v) for k, v in inputs.items()}
    col = lambda v: v.reshape(-1, 1)
    laid = [
        ("x", a["x"]), ("wqk_t", a["Wqk_t"]), ("wv_t", a["Wv_t"]), ("wo_t", a["Wo_t"]), ("tau_t", a["tau_t"].reshape(-1)),
        ("wqk_c", a["Wqk_c"]), ("wvT_c", a["Wv_c"].T), ("wo_c", a["Wo_c"]),
        ("tau_c", col(_np.repeat(a["tau_c"].reshape(-1), CDH))),
        ("ln1_w", col(a["ln1_w"])), ("ln1_b", col(a["ln1_b"])), ("ln2_w", col(a["ln2_w"])), ("ln2_b", col(a["ln2_b"])),
        ("gamma1", a["gamma1"]), ("gamma2", a["gamma2"]), ("switch_w", a["switch_w"]), ("switch_b", a["switch_b"]),
        ("w1", a["w1"]), ("b1T", a["b1"].reshape(E * FT, P).T), ("w2", a["w2"]), ("b2", a["b2"]),
    ]
    nc = _bacc.Bacc("TRN2", target_bir_lowering=False, num_devices=1)
    arrays, args = {}, []
    for name, v in laid:
        v = _np.ascontiguousarray(v)
        arrays[f"in_{name}"] = v
        args.append(nc.dram_tensor(f"in_{name}", v.shape, _mybir.dt.from_np(v.dtype), kind="ExternalInput").ap())
    args.append(nc.dram_tensor("out_0", (B, N, D), F32, kind="ExternalOutput").ap())
    build(nc, *args)
    r = _run(nc, [arrays], core_ids=[0])
    return r.results[0]["out_0"]
```
